# Optimizing a Trainium2 kernel written in Bass

```python
import numpy as np
import jax
import jax.numpy as jnp

def _softmax(x, axis=-1):
    return jax.nn.softmax(x, axis=axis)

def _gelu(x):
    return jax.nn.gelu(x, approximate=True)

def _silu(x):
    return jax.nn.silu(x)

def _sigmoid(x):
    return jax.nn.sigmoid(x)

def _layernorm(x, axis=-1, eps=1e-05):
    m = jnp.mean(x, axis=axis, keepdims=True)
    v = jnp.var(x, axis=axis, keepdims=True)
    return (x - m) / jnp.sqrt(v + eps)

def _scatter_add(tgt, idx, src, axis=0):
    return tgt.at[idx].add(src)

def _segment_sum(src, seg, n):
    return jax.ops.segment_sum(src, seg, n)
kernel_name = 'mk_macaron_d2_jaxref_r8_3ea459'

def setup_inputs(seed: int=0):
    np.random.seed(seed)
    _w = jnp.asarray

    def _L0_attn_setup():
        import jax, jax.numpy as jnp
        import numpy as np
        import math
        NUM_HEADS = 16
        ROPE_BASE = 10000.0

        def _rope_cos_sin(seq_len, head_dim, dtype):
            half = head_dim // 2
            inv_freq = 1.0 / ROPE_BASE ** (jnp.arange(0, head_dim, 2, dtype=jnp.float32) / head_dim)
            t = jnp.arange(seq_len, dtype=jnp.float32)
            freqs = jnp.einsum('i,j->ij', t, inv_freq)
            cos = jnp.cos(freqs).astype(dtype)[None, None]
            sin = jnp.sin(freqs).astype(dtype)[None, None]
            return (cos, sin)

        def _apply_rope(x, cos, sin):
            half = x.shape[-1] // 2
            x1, x2 = (x[..., :half], x[..., half:])
            return jnp.concatenate([x1 * cos - x2 * sin, x2 * cos + x1 * sin], axis=-1)
        key = jax.random.key(seed)
        ks = jax.random.split(key, 5)
        B, S, H = (2, 256, 256)
        scale = 1.0 / math.sqrt(H)
        return {'hidden_states': jax.random.normal(ks[0], (B, S, H), dtype=jnp.float32), 'Wq': jax.random.normal(ks[1], (H, H), dtype=jnp.float32) * scale, 'Wk': jax.random.normal(ks[2], (H, H), dtype=jnp.float32) * scale, 'Wv': jax.random.normal(ks[3], (H, H), dtype=jnp.float32) * scale, 'Wo': jax.random.normal(ks[4], (H, H), dtype=jnp.float32) * scale}
    _L0_attn_in = _L0_attn_setup()

    def _L0_ffn_setup():
        import jax, jax.numpy as jnp
        import numpy as np
        DIM = 256
        HID = 704
        ZERO_POINT = 128.0

        def _qlinear(x, wq, scale):
            W = (wq.astype(jnp.float32) - ZERO_POINT) * scale[:, None]
            return jnp.einsum('bsd,hd->bsh', x, W)
        key = jax.random.key(seed)
        ks = jax.random.split(key, 7)
        B, S = (4, 256)
        sg = jax.random.uniform(ks[1], (HID,)) * (0.02 / np.sqrt(DIM)) + 0.0001
        su = jax.random.uniform(ks[3], (HID,)) * (0.02 / np.sqrt(DIM)) + 0.0001
        sd = jax.random.uniform(ks[5], (DIM,)) * (0.02 / np.sqrt(HID)) + 0.0001
        return {'x': jax.random.normal(ks[0], (B, S, DIM), dtype=jnp.float32), 'wq_gate': jax.random.randint(ks[2], (HID, DIM), 0, 32, dtype=jnp.int32), 's_gate': sg, 'wq_up': jax.random.randint(ks[4], (HID, DIM), 0, 32, dtype=jnp.int32), 's_up': su, 'wq_down': jax.random.randint(ks[6], (DIM, HID), 0, 32, dtype=jnp.int32), 's_down': sd}
    _L0_ffn_in = _L0_ffn_setup()

    def _L1_attn_setup():
        import jax, jax.numpy as jnp
        import numpy as np
        B, T, C = (2, 256, 256)
        H, KVH = (16, 4)
        HD = C // H
        REP = H // KVH

        def _alibi_slopes(n_head):
            start = 2.0 ** (-2.0 ** (-(np.log2(n_head) - 3.0)))
            return jnp.asarray([start ** (i + 1) for i in range(n_head)], jnp.float32)
        key = jax.random.key(seed)
        ks = jax.random.split(key, 4)
        sc = 0.02
        return {'x': jax.random.normal(ks[0], (B, T, C), jnp.float32), 'Wq': jax.random.normal(ks[1], (C, C), jnp.float32) * sc, 'Wkv': jax.random.normal(ks[2], (C, HD * KVH * 2), jnp.float32) * sc, 'Wo': jax.random.normal(ks[3], (C, C), jnp.float32) * sc, 'bo': jnp.zeros((C,), jnp.float32)}
    _L1_attn_in = _L1_attn_setup()

    def _L1_ffn_setup():
        import jax, jax.numpy as jnp
        import numpy as np
        EPS = 1e-08

        def _quantize(w):
            gamma = jnp.mean(jnp.abs(w))
            return jnp.clip(jnp.round(w / (gamma + EPS)), -1.0, 1.0)

        def _bitlinear(x, w):
            return jnp.matmul(x, _quantize(w).T)
        key = jax.random.key(seed)
        k1, k2, k3, k4 = jax.random.split(key, 4)
        d, h = (256, 704)
        x = jax.random.normal(k1, (4, 256, d), dtype=jnp.float32)
        w1 = jax.random.normal(k2, (h, d), dtype=jnp.float32)
        w2 = jax.random.normal(k3, (h, d), dtype=jnp.float32)
        w3 = jax.random.normal(k4, (d, h), dtype=jnp.float32)
        return {'x': x, 'w1': w1, 'w2': w2, 'w3': w3}
    _L1_ffn_in = _L1_ffn_setup()
    _d = {'L0_attn_hidden_states': _L0_attn_in['hidden_states'], 'L0_attn_Wq': _L0_attn_in['Wq'], 'L0_attn_Wk': _L0_attn_in['Wk'], 'L0_attn_Wv': _L0_attn_in['Wv'], 'L0_attn_Wo': _L0_attn_in['Wo'], 'L0_ffn_wq_gate': _L0_ffn_in['wq_gate'], 'L0_ffn_s_gate': _L0_ffn_in['s_gate'], 'L0_ffn_wq_up': _L0_ffn_in['wq_up'], 'L0_ffn_s_up': _L0_ffn_in['s_up'], 'L0_ffn_wq_down': _L0_ffn_in['wq_down'], 'L0_ffn_s_down': _L0_ffn_in['s_down'], 'L1_attn_Wq': _L1_attn_in['Wq'], 'L1_attn_Wkv': _L1_attn_in['Wkv'], 'L1_attn_Wo': _L1_attn_in['Wo'], 'L1_attn_bo': _L1_attn_in['bo'], 'L1_ffn_w1': _L1_ffn_in['w1'], 'L1_ffn_w2': _L1_ffn_in['w2'], 'L1_ffn_w3': _L1_ffn_in['w3']}
    _x0 = _d['L0_attn_hidden_states']
    _d['L0_attn_hidden_states'] = jax.random.normal(jax.random.fold_in(jax.random.key(seed), 1), (4, 512, 256), dtype=_x0.dtype)
    del _x0
    return _d

def reference(L0_attn_hidden_states, L0_attn_Wq, L0_attn_Wk, L0_attn_Wv, L0_attn_Wo, L0_ffn_wq_gate, L0_ffn_s_gate, L0_ffn_wq_up, L0_ffn_s_up, L0_ffn_wq_down, L0_ffn_s_down, L1_attn_Wq, L1_attn_Wkv, L1_attn_Wo, L1_attn_bo, L1_ffn_w1, L1_ffn_w2, L1_ffn_w3):

    def _L0_attn_ref(hidden_states, Wq, Wk, Wv, Wo):
        import jax, jax.numpy as jnp
        import numpy as np
        import math
        NUM_HEADS = 16
        ROPE_BASE = 10000.0

        def _rope_cos_sin(seq_len, head_dim, dtype):
            half = head_dim // 2
            inv_freq = 1.0 / ROPE_BASE ** (jnp.arange(0, head_dim, 2, dtype=jnp.float32) / head_dim)
            t = jnp.arange(seq_len, dtype=jnp.float32)
            freqs = jnp.einsum('i,j->ij', t, inv_freq)
            cos = jnp.cos(freqs).astype(dtype)[None, None]
            sin = jnp.sin(freqs).astype(dtype)[None, None]
            return (cos, sin)

        def _apply_rope(x, cos, sin):
            half = x.shape[-1] // 2
            x1, x2 = (x[..., :half], x[..., half:])
            return jnp.concatenate([x1 * cos - x2 * sin, x2 * cos + x1 * sin], axis=-1)
        B, S, H = hidden_states.shape
        nh = NUM_HEADS
        hd = H // nh

        def proj(W):
            y = jnp.einsum('bsh,oh->bso', hidden_states, W)
            return y.reshape(B, S, nh, hd).transpose(0, 2, 1, 3)
        q, k, v = (proj(Wq), proj(Wk), proj(Wv))
        cos, sin = _rope_cos_sin(S, hd, hidden_states.dtype)
        q = _apply_rope(q, cos, sin)
        k = _apply_rope(k, cos, sin)
        scores = jnp.einsum('bhqd,bhkd->bhqk', q, k) / math.sqrt(hd)
        causal = jnp.triu(jnp.full((S, S), -jnp.inf, dtype=scores.dtype), k=1)
        scores = scores + causal[None, None]
        probs = jax.nn.softmax(scores, axis=-1)
        ctx = jnp.einsum('bhqk,bhkd->bhqd', probs, v)
        ctx = ctx.transpose(0, 2, 1, 3).reshape(B, S, H)
        out = jnp.einsum('bsh,oh->bso', ctx, Wo)
        return out

    def _L0_ffn_ref(x, wq_gate, s_gate, wq_up, s_up, wq_down, s_down):
        import jax, jax.numpy as jnp
        import numpy as np
        DIM = 256
        HID = 704
        ZERO_POINT = 128.0

        def _qlinear(x, wq, scale):
            W = (wq.astype(jnp.float32) - ZERO_POINT) * scale[:, None]
            return jnp.einsum('bsd,hd->bsh', x, W)
        gate = _qlinear(x, wq_gate, s_gate)
        gate = jax.nn.silu(gate)
        up = _qlinear(x, wq_up, s_up)
        return _qlinear(gate * up, wq_down, s_down)

    def _L1_attn_ref(x, Wq, Wkv, Wo, bo):
        import jax, jax.numpy as jnp
        import numpy as np
        B, T, C = (2, 256, 256)
        H, KVH = (16, 4)
        HD = C // H
        REP = H // KVH

        def _alibi_slopes(n_head):
            start = 2.0 ** (-2.0 ** (-(np.log2(n_head) - 3.0)))
            return jnp.asarray([start ** (i + 1) for i in range(n_head)], jnp.float32)
        Bv, Tv, Cv = x.shape
        q = (x @ Wq).reshape(Bv, Tv, H, HD).transpose(0, 2, 1, 3)
        k, v = jnp.split(x @ Wkv, 2, axis=-1)
        k = k.reshape(Bv, Tv, KVH, HD).transpose(0, 2, 1, 3)
        v = v.reshape(Bv, Tv, KVH, HD).transpose(0, 2, 1, 3)
        qg = q.reshape(Bv, REP, KVH, Tv, HD)
        scores = jnp.einsum('brgtd,bgsd->brgts', qg, k) / jnp.sqrt(jnp.float32(HD))
        idx = jnp.arange(Tv)
        diff = (idx[None, :] - idx[:, None]).astype(jnp.float32)
        slopes = _alibi_slopes(H).reshape(REP, KVH)
        bias = jnp.tril(diff)[None, None] * slopes[:, :, None, None]
        causal = idx[None, :] <= idx[:, None]
        scores = jnp.where(causal[None, None, None], scores + bias[None], -jnp.inf)
        attn = jax.nn.softmax(scores, axis=-1)
        out = jnp.einsum('brgts,bgsd->brgtd', attn, v)
        out = out.reshape(Bv, H, Tv, HD).transpose(0, 2, 1, 3).reshape(Bv, Tv, Cv)
        return out @ Wo + bo

    def _L1_ffn_ref(x, w1, w2, w3):
        import jax, jax.numpy as jnp
        import numpy as np
        EPS = 1e-08

        def _quantize(w):
            gamma = jnp.mean(jnp.abs(w))
            return jnp.clip(jnp.round(w / (gamma + EPS)), -1.0, 1.0)

        def _bitlinear(x, w):
            return jnp.matmul(x, _quantize(w).T)
        x1 = _bitlinear(x, w1)
        x2 = _bitlinear(x, w2)
        hidden = jax.nn.sigmoid(x1) * x2
        return _bitlinear(hidden, w3)
    x = L0_attn_hidden_states
    x = x + 0.5 * _L0_ffn_ref(_layernorm(x, axis=-1), L0_ffn_wq_gate, L0_ffn_s_gate, L0_ffn_wq_up, L0_ffn_s_up, L0_ffn_wq_down, L0_ffn_s_down)
    x = x + _L0_attn_ref(_layernorm(x, axis=-1), L0_attn_Wq, L0_attn_Wk, L0_attn_Wv, L0_attn_Wo)
    x = x + 0.5 * _L0_ffn_ref(_layernorm(x, axis=-1), L0_ffn_wq_gate, L0_ffn_s_gate, L0_ffn_wq_up, L0_ffn_s_up, L0_ffn_wq_down, L0_ffn_s_down)
    x = x + 0.5 * _L1_ffn_ref(_layernorm(x, axis=-1), L1_ffn_w1, L1_ffn_w2, L1_ffn_w3)
    x = x + _L1_attn_ref(_layernorm(x, axis=-1), L1_attn_Wq, L1_attn_Wkv, L1_attn_Wo, L1_attn_bo)
    x = x + 0.5 * _L1_ffn_ref(_layernorm(x, axis=-1), L1_ffn_w1, L1_ffn_w2, L1_ffn_w3)
    return x

_drawn_inputs = setup_inputs


def setup_inputs(seed=0):
    import zlib

    import numpy as np

    out = dict(_drawn_inputs(seed))
    spreads = {'L1_attn_bo': (0.0, 0.8)}
    factors = {'L0_ffn_s_gate': 8.0,
     'L0_ffn_s_up': 8.0,
     'L0_ffn_s_down': 5.308,
     'L1_attn_Wq': 8.0,
     'L1_attn_Wkv': 8.0,
     'L1_attn_Wo': 8.0}
    for name, (base, spread) in spreads.items():
        noise = np.random.default_rng([zlib.crc32(name.encode()), seed]).standard_normal(out[name].shape)
        drawn = base * np.exp(spread * noise) if base else spread * noise
        out[name] = jnp.asarray(drawn.astype(out[name].dtype))
    for name, factor in factors.items():
        out[name] = (out[name] * factor).astype(out[name].dtype)
    return out
```

```python
import concourse.bass as bass
from concourse import mybir
from contextlib import ExitStack

F32 = mybir.dt.float32
F16 = mybir.dt.float16
BF16 = mybir.dt.bfloat16
I32 = mybir.dt.int32
ACT = mybir.ActivationFunctionType
ALU = mybir.AluOpType
AX = mybir.AxisListType

P = 128
NB = 4
T = 512
NT = 4
D = 256
HID = 704
NH = 16
FC = 6
XS = 16.0
HS = 16.0
WS = 64.0
CS = 16.0
QROWS = 97


class Queue:

    def __init__(self, name, sem):
        self.name, self.sem, self.count, self.items, self.seen = name, sem, 0, [], {}

    def wait(self, tokens):
        for t in tokens:
            if t is None:
                continue
            if isinstance(t, list):
                self.wait(t)
                continue
            sem, value = t
            if self.seen.get(id(sem), 0) < value:
                self.seen[id(sem)] = value
                self.items.append(lambda e, s=sem, v=value: e.wait_ge(s, v))

    def do(self, fn, *after, inc=True):
        self.wait(after)
        if not inc:
            self.items.append(fn)
            return None
        self.count += 1
        self.items.append(lambda e, f=fn: f(e).then_inc(self.sem, 1))
        return (self.sem, self.count)

    def dma(self, out, in_, group, *after):
        self.wait(after)
        group.count += 16
        self.items.append(lambda e, s=group.sem: e.dma_start(out, in_).then_inc(s, 16))

    def replay(self, e):
        for f in self.items:
            f(e)


class Group:

    def __init__(self, sem):
        self.sem, self.count = sem, 0

    @property
    def done(self):
        return (self.sem, self.count)


class Ring:

    def __init__(self, bufs):
        self.bufs = bufs
        self.idle = [(i, []) for i in range(len(bufs))]

    def take(self):
        i, after = self.idle.pop(0)
        return i, self.bufs[i], after

    def free(self, i, *tokens):
        self.idle.append((i, list(tokens)))


def interleave(*streams):
    live = [[0.0, w, g] for w, g in streams]
    while live:
        s = min(live, key=lambda r: r[0] / r[1])
        try:
            s[0] += next(s[2])
        except StopIteration:
            live.remove(s)


def macaron_kernel(nc, x_in, wqkv0, wo0, gu0, sgu0, wd0, sd0, wqkv1, wo1, gu1, wd1,
                   rope, mask, ident, identh, alibi_q, alibi_k, scratch, out):
    ctx = ExitStack()
    with ctx:
        def sb(name, shape, dt=F32):
            return ctx.enter_context(nc.sbuf_tensor(name, shape, dt))

        def sem(name):
            return ctx.enter_context(nc.semaphore(name))

        X = sb("X", [P, NB * NT, D])
        WGU = [sb(f"WGU{l}", [P, 2, 2 * HID], F16) for l in range(2)]
        WD = [sb(f"WD{l}", [P, FC, D], F16) for l in range(2)]
        SGU = sb("SGU", [P, 2, FC])
        SGH = sb("SGH", [P, FC])
        SUH = sb("SUH", [P, FC])
        SD = sb("SD", [P, D])
        NQKV = [768, 384]
        WA = [sb(f"WA{l}", [P, 2, 2, NQKV[l]], F16) for l in range(2)]
        WO = [sb(f"WO{l}", [P, 2, 4, D], F16) for l in range(2)]
        ROPE = sb("ROPE", [P, 2, T])
        MASK = sb("MASK", [P, 2, P], BF16)
        ID = sb("ID", [P, P])
        IDH = sb("IDH", [P, P], BF16)
        ONE = sb("ONE", [P, P])
        LN = [[sb(f"XN{i}", [P, NT, D]), sb(f"ST{i}", [P, NT, 6]), sb(f"MV{i}", [P, NT, 2]),
               sb(f"VE{i}", [P, NT]), sb(f"YR{i}", [P, NT]), sb(f"AR{i}", [P, NT])] for i in range(2)]
        XT = [[sb(f"XT{i}{j}", [P, 2, T], F16) for j in range(2)] for i in range(2)]
        TH = sb("TH", [P, 2, T])
        HH = [sb(f"HH{j}", [P, FC, T], F16) for j in range(2)]
        DT = sb("DT", [P, 2, T])
        QF = sb("QF", [P, 2, T])
        QS = sb("QS", [P, 2, T])
        QP = [sb(f"QP{j}", [P, 4, T], F16) for j in range(2)]
        SQ = sb("SQ", [QROWS, NH, T], F16)
        SK = sb("SK", [QROWS, NH, T], F16)
        V = sb("V", [P, NT, NH, 32])
        MX = sb("MX", [P, 4, 4, NT])
        NM = sb("NM", [16, 4, P], F16)
        PB = [sb(f"PB{i}", [P, 2, 5 * T]) for i in range(2)]
        OT = sb("OT", [P, 4, T])
        DC = sb("DC", [P, 64])
        RB = sb("RB", [P, 4, T])
        CH = QP
        GA = sb("GA", [P, 3, 22])
        GS = sb("GS", [P, 6])
        TB = QP[1][:, :, :].rearrange("p c t -> p (c t)")

        banks = [ctx.enter_context(nc.psum_tensor(f"B{i}", [P, T], F32)) for i in range(8)]
        DENSE = Ring(banks[0:3])
        MAXB = Ring(banks[3:5])
        STB = Ring(banks[5:7])
        PVB = Ring(banks[7:8])

        pe = Queue("pe", sem("s_pe"))
        ve = Queue("ve", sem("s_ve"))
        ac = Queue("ac", sem("s_ac"))
        po = Queue("po", sem("s_po"))
        sp = Queue("sp", None)
        stores = []

        def group(name):
            return Group(sem(name))

        g_const = group("g_const")
        sp.dma(X[:, 0:NT, :], x_in[:, 0:NT, :], g_const)
        sp.dma(ID[:, :], ident, g_const)
        g_w0 = group("g_w0")
        raw = [PB[l][:, :, :].rearrange("p a n -> p (a n)") for l in range(2)]
        rawi = raw[0][:, 0:4 * HID + FC * D].bitcast(I32)
        rgu = raw[1][:, 0:4 * HID].rearrange("p (k n) -> p k n", k=2)
        rd = raw[1][:, 4 * HID:4 * HID + FC * D].rearrange("p (c n) -> p c n", c=FC)
        rgui = rawi[:, 0:4 * HID].rearrange("p (k n) -> p k n", k=2)
        rdi = rawi[:, 4 * HID:].rearrange("p (c n) -> p c n", c=FC)
        sp.dma(rgui, gu0, g_w0)
        sp.dma(rdi, wd0, g_w0)
        sp.dma(SGU[:, :, :], sgu0, g_w0)
        sp.dma(SD[:, :], sd0, g_w0)
        g_x = group("g_x")
        sp.dma(X[:, NT:, :], x_in[:, NT:, :], g_x)
        g_a0 = group("g_a0")
        ra = [OT[:, 0:3, :].rearrange("p g t -> p (g t)").rearrange("p (k n) -> p k n", k=2),
              raw[0][:, 4 * HID + FC * D:].rearrange("p (k n) -> p k n", k=2)]
        ro = [RB[:, 0:2, :].rearrange("p g t -> p (g t)").rearrange("p (c n) -> p c n", c=4),
              QP[0][:, :, :].rearrange("p c t -> p (c t)").bitcast(F32).rearrange("p (c n) -> p c n", c=4)]
        sp.dma(ra[0], wqkv0, g_a0)
        sp.dma(ro[0], wo0, g_a0)
        g_c2 = group("g_c2")
        sp.dma(ROPE[:, :, :], rope, g_c2)
        sp.dma(MASK[:, :, :], mask, g_c2)
        sp.dma(IDH[:, :], identh, g_c2)

        z_sq = po.do(lambda e: e.memset(SQ[:, :, :], 0.0))
        z_sk = po.do(lambda e: e.memset(SK[:, :, :], 0.0))
        z_k1 = po.do(lambda e: e.memset(SK[96:97, :, :], 1.0), z_sk)
        z_v = po.do(lambda e: e.memset(V[:, :, :, 16:32], 1.0), z_k1)
        z_one = po.do(lambda e: e.memset(ONE[:, :], 1.0))

        w_gu0 = ve.do(lambda e: e.tensor_scalar(WGU[0][:, :, :], rgui, -128.0, None, ALU.add), g_w0.done)
        w_d0 = ve.do(lambda e: e.tensor_scalar(WD[0][:, :, :], rdi, -128.0, None, ALU.add))
        w_sg = ve.do(lambda e: e.tensor_scalar(SGH[:, :], SGU[:, 0, :], 0.5 / XS, None, ALU.mult))
        w_su = ve.do(lambda e: e.scalar_tensor_tensor(SUH[:, :], SGU[:, 0, :], 0.5 * HS / (XS * XS),
                                                      SGU[:, 1, :], ALU.mult, ALU.mult))
        w_ffn = [[w_gu0, w_d0, w_sg, w_su], None]

        def attention_weights(l, loaded):
            n = NQKV[l]
            hi = ac.do(lambda e: e.activation(WA[l][:, 0, :, :], ra[l], ACT.Copy, scale=WS), loaded)
            lo = ve.do(lambda e: e.scalar_tensor_tensor(WA[l][:, 1, :, :], ra[l], WS, WA[l][:, 0, :, :],
                                                        ALU.mult, ALU.subtract), hi, loaded)
            ohi = ac.do(lambda e: e.activation(WO[l][:, 0, :, :], ro[l], ACT.Copy, scale=WS))
            olo = ve.do(lambda e: e.scalar_tensor_tensor(WO[l][:, 1, :, :], ro[l], WS, WO[l][:, 0, :, :],
                                                         ALU.mult, ALU.subtract), ohi)
            return [hi, lo, ohi, olo]

        w_att = [None, None]
        zeroed = []

        def ternary_weights():
            g = group("g_w1")
            sp.dma(rgu, gu1, g)
            sp.dma(rd, wd1, g)
            for i in range(2):
                a = ve.do(lambda e, i=i: e.tensor_reduce(
                    GA[:, i, :].rearrange("p (k a) -> p k a", k=2),
                    rgu[:, :, i * HID:(i + 1) * HID].rearrange("p k (a b) -> p k a b", b=64),
                    AX.X, ALU.add, apply_absolute_value=True), g.done)
            yield 300
            b = ve.do(lambda e: e.tensor_reduce(GA[:, 2, 0:20], rd[:, 0:5, :].rearrange("p c (a b) -> p (c a) b", b=64),
                                                AX.X, ALU.add, apply_absolute_value=True))
            c = ve.do(lambda e: e.tensor_reduce(GA[:, 2, 20:21], rd[0:P, 5:6, :], AX.XY, ALU.add,
                                                apply_absolute_value=True))
            c2 = ve.do(lambda e: e.tensor_scalar(GA[:, 2, 21:22], GA[:, 2, 20:21], -0.5, None, ALU.mult), c)
            d = ve.do(lambda e: e.tensor_reduce(GS[:, 0:3], GA[:, :, :], AX.X, ALU.add), a, b, c2)
            i, bank, after = DENSE.take()
            m = pe.do(lambda e: e.matmul(bank[:, 0:3], ONE[:, :], GS[:, 0:3], start=True, stop=True), d, z_one, after)
            th = ve.do(lambda e: e.tensor_scalar(GS[:, 0:3], bank[:, 0:3], 1.0 / (HID * D), 1e-8, ALU.mult, ALU.add), m)
            DENSE.free(i, th)
            t5 = ve.do(lambda e: e.tensor_scalar(GS[:, 3:6], GS[:, 0:3], -0.5, None, ALU.mult), th)
            t6 = ve.do(lambda e: e.tensor_scalar(GS[:, 0:3], GS[:, 0:3], 0.5, None, ALU.mult), t5)
            yield 300
            last, got = None, []
            for k in range(2):
                u = []
                for i in range(2):
                    u.append(ve.do(lambda e, k=k, i=i: e.tensor_scalar(
                        TB[:, i * HID:(i + 1) * HID], rgu[:, k, i * HID:(i + 1) * HID],
                        GS[:, 3 + i:4 + i], None, ALU.is_lt), t6, last))
                for i in range(2):
                    last = ve.do(lambda e, k=k, i=i: e.scalar_tensor_tensor(
                        WGU[1][:, k, i * HID:(i + 1) * HID], rgu[:, k, i * HID:(i + 1) * HID], GS[:, i:i + 1],
                        TB[:, i * HID:(i + 1) * HID], ALU.is_gt, ALU.subtract), u)
                got.append(last)
                yield 300
            for k in range(2):
                src = rd[:, 3 * k:3 * k + 3, :].rearrange("p c n -> p (c n)")
                u = ve.do(lambda e, s=src: e.tensor_scalar(TB[:, 0:768], s, GS[:, 5:6], None, ALU.is_lt), last)
                last = ve.do(lambda e, s=src, k=k: e.scalar_tensor_tensor(
                    WD[1][:, 3 * k:3 * k + 3, :].rearrange("p c n -> p (c n)"), s, GS[:, 2:3], TB[:, 0:768],
                    ALU.is_gt, ALU.subtract), u)
                got.append(last)
            w_ffn[1] = got
            yield 300

        XTR = Ring(XT)
        x_ready = [[g_const.done]] + [[g_const.done, g_x.done] for _ in range(3)]
        LNR = Ring(LN)

        def layer_norm(b, lag):
            slot, (XN, ST6, MV, VE, YR, AR), after_ln = LNR.take()
            st = [ve.do(lambda e, i=i: e.bn_stats(ST6[:, i, :], X[:, NT * b + i, :]), x_ready[b], after_ln)
                  for i in range(NT)]
            mv = [ve.do(lambda e, i=i: e.bn_aggr(MV[:, i, :], ST6[:, i, :]), st[i]) for i in range(NT)]
            q = ve.do(lambda e: e.tensor_scalar(VE[:, :], MV[:, :, 1], 1e-5, 1.0 / (XS * XS), ALU.add, ALU.mult), mv)
            s = ve.do(lambda e: e.tensor_scalar(AR[:, :].bitcast(I32), VE[:, :].bitcast(I32), 1, None,
                                                ALU.logical_shift_right), q)
            y = ve.do(lambda e: e.tensor_scalar(YR[:, :].bitcast(I32), AR[:, :].bitcast(I32), -1.0, 1597463007.0,
                                                ALU.mult, ALU.add), s)
            for _ in range(3):
                a = ve.do(lambda e: e.scalar_tensor_tensor(AR[:, :], YR[:, :], -0.5, YR[:, :], ALU.mult, ALU.mult), y)
                a = ve.do(lambda e: e.tensor_tensor(AR[:, :], AR[:, :], VE[:, :], ALU.mult), a)
                y = ve.do(lambda e: e.scalar_tensor_tensor(YR[:, :], AR[:, :], 1.5, YR[:, :], ALU.add, ALU.mult), a)
            xn = [po.do(lambda e, i=i: e.tensor_scalar(XN[:, i, :], X[:, NT * b + i, :], MV[:, i, 0:1], YR[:, i:i + 1],
                                                       ALU.subtract, ALU.mult), y) for i in range(NT)]
            yield lag
            n, xt, after_xt = XTR.take()
            parts, trs = [], []
            for k in range(2):
                i, bank, after = DENSE.take()
                for t in range(NT):
                    tr = pe.do(lambda e, k=k, t=t, bank=bank: e.transpose(
                        bank[:, t * P:(t + 1) * P], XN[:, t, k * P:(k + 1) * P], ID[:, :]),
                        xn[t], g_const.done, after, inc=t == NT - 1)
                trs.append(tr)
                hi = ac.do(lambda e, k=k, bank=bank: e.activation(xt[0][:, k, :], bank[:, :], ACT.Copy), tr, after_xt)
                lo = ve.do(lambda e, k=k, bank=bank: e.tensor_tensor(xt[1][:, k, :], bank[:, :], xt[0][:, k, :],
                                                                    ALU.subtract), hi, after_xt)
                DENSE.free(i, hi, lo)
                parts += [hi, lo]
                yield 440
            LNR.free(slot, trs, xn[-1])
            return n, xt, parts, xn

        H2 = Ring([0, 1])
        D2 = Ring([0, 1])
        ffn_free = {"HH": []}

        def ffn(b, l):
            n, xt, x_parts, x_read = yield from layer_norm(b, 2500)
            ready = []
            for c in range(FC):
                half = c == FC - 1
                w = T // 2 if half else T
                got = []
                for u in range(2):
                    i, bank, after = DENSE.take()
                    for j in range(2):
                        for k in range(2):
                            col = u * HID + c * P
                            first, last = j == 0 and k == 0, j == 1 and k == 1
                            if half:
                                for z in range(2):
                                    m = pe.do(lambda e, z=z, j=j, k=k, col=col, bank=bank, first=first, last=last:
                                              e.matmul(bank[64 * z:64 * z + 64, 0:256], WGU[l][:, k, col:col + 64],
                                                       xt[j][:, k, 256 * z:256 * z + 256], start=first, stop=last),
                                              x_parts, w_ffn[l], after, inc=last and z == 1)
                            else:
                                m = pe.do(lambda e, j=j, k=k, col=col, bank=bank, first=first, last=last:
                                          e.matmul(bank[:, :], WGU[l][:, k, col:col + P], xt[j][:, k, :],
                                                   start=first, stop=last),
                                          x_parts, w_ffn[l], after, inc=last)
                    got.append((i, bank, m))
                (ig, bg, mg), (iu, bu, mu) = got
                r, _, after_h = H2.take()
                if l == 0:
                    th = ac.do(lambda e, c=c, r=r, bg=bg, w=w: e.activation(TH[:, r, 0:w], bg[:, 0:w], ACT.Tanh,
                                                                            scale=SGH[:, c:c + 1]), mg, after_h)
                    t1 = ve.do(lambda e, r=r, bg=bg, w=w: e.scalar_tensor_tensor(
                        TH[:, r, 0:w], TH[:, r, 0:w], 1.0, bg[:, 0:w], ALU.add, ALU.mult), th, mg, after_h)
                    h = ve.do(lambda e, c=c, r=r, bu=bu, w=w: e.scalar_tensor_tensor(
                        TH[:, r, 0:w], bu[:, 0:w], SUH[:, c:c + 1], TH[:, r, 0:w], ALU.mult, ALU.mult), mu, t1)
                    DENSE.free(ig, th, t1)
                else:
                    th = ac.do(lambda e, r=r, bg=bg, w=w: e.activation(TH[:, r, 0:w], bg[:, 0:w], ACT.Tanh,
                                                                       scale=0.5 / XS), mg, after_h)
                    h = ve.do(lambda e, r=r, bu=bu, w=w: e.scalar_tensor_tensor(
                        TH[:, r, 0:w], TH[:, r, 0:w], 1.0, bu[:, 0:w], ALU.add, ALU.mult), th, mu, after_h)
                    DENSE.free(ig, th)
                DENSE.free(iu, h)
                hi = ac.do(lambda e, c=c, r=r, w=w: e.activation(HH[0][:, c, 0:w], TH[:, r, 0:w], ACT.Copy),
                           h, ffn_free["HH"])
                lo = po.do(lambda e, c=c, r=r, w=w: e.tensor_tensor(HH[1][:, c, 0:w], TH[:, r, 0:w],
                                                                   HH[0][:, c, 0:w], ALU.subtract), hi, h)
                H2.free(r, lo, hi)
                ready += [hi, lo]
                yield 870 if half else 1740
            XTR.free(n, mu)
            yield 1500
            new = []
            for pair in range(2):
                i, bank, after = DENSE.take()
                for q in range(2):
                    t = 2 * pair + q
                    z = t // 2
                    steps = [(c, j) for c in range(FC) for j in range(2)]
                    for s, (c, j) in enumerate(steps):
                        if c < FC - 1:
                            lhs, rhs = HH[j][:, c, t * P:(t + 1) * P], WD[l][:, c, :]
                        else:
                            lhs = HH[j][64 * z:64 * z + 64, c, (t % 2) * P:(t % 2 + 1) * P]
                            rhs = WD[l][64 * z:64 * z + 64, c, :]
                        m = pe.do(lambda e, lhs=lhs, rhs=rhs, bank=bank, q=q, s=s:
                                  e.matmul(bank[:, q * D:(q + 1) * D], lhs, rhs, start=s == 0, stop=s == 11),
                                  ready, w_ffn[l], after, inc=s == 11)
                xv = X[:, NT * b + 2 * pair:NT * b + 2 * pair + 2, :].rearrange("p t n -> p (t n)")
                if l == 0:
                    r, _, after_d = D2.take()
                    sdb = SD[:, :].unsqueeze(1).to_broadcast([P, 2, D])
                    d = ve.do(lambda e, r=r, bank=bank, sdb=sdb: e.scalar_tensor_tensor(
                        DT[:, r, :].rearrange("p (t n) -> p t n", t=2), bank[:, :].rearrange("p (t n) -> p t n", t=2),
                        0.5 / HS, sdb, ALU.mult, ALU.mult), m, after_d)
                    DENSE.free(i, d)
                    y = po.do(lambda e, r=r, xv=xv: e.tensor_tensor(xv, xv, DT[:, r, :], ALU.add), d, x_read)
                    D2.free(r, y)
                else:
                    y = ve.do(lambda e, xv=xv, bank=bank: e.scalar_tensor_tensor(
                        xv, bank[:, :], 0.25 / XS, xv, ALU.mult, ALU.add), m, x_read)
                    DENSE.free(i, y)
                new.append(y)
                yield 2700
            ffn_free["HH"] = [m]
            x_ready[b] = new

        Q2 = Ring([0, 1])
        PR = Ring(PB)
        free = {k: [] for k in ("QP", "SQ", "SQM", "SK", "V", "MX", "NM", "OT", "DC", "RB", "CH", "SCR")}
        consts = {"alibi": None}
        TERMS = [(0, 0), (0, 1), (1, 0)]

        def attention(b, l):
            KH = NH if l == 0 else 4
            n, xt, x_parts, x_read = yield from layer_norm(b, 2500)
            inv = 1.0 / (XS * WS)
            g_st = group(f"g_st{l}{b}")

            def project(cols, width, w):
                i, bank, after = DENSE.take()
                for s, (jw, jx) in enumerate(TERMS):
                    for k in range(2):
                        m = pe.do(lambda e, jw=jw, jx=jx, k=k, s=s: e.matmul(
                            bank[0:width, :], WA[l][:, jw, k, cols:cols + width], xt[jx][:, k, :],
                            start=s == 0 and k == 0, stop=s == 2 and k == 1),
                            x_parts, w, after, inc=s == 2 and k == 1)
                return i, bank, m

            nq = 4 if l == 0 else 3
            parts = []
            for c in range(nq):
                width = 64 if (l == 1 and c == 2) else P
                i, bank, m = project(c * P, width, w_att[l])
                if l == 0:
                    r, _, after_q = Q2.take()
                    qf = ac.do(lambda e, r=r, bank=bank: e.activation(QF[:, r, :], bank[:, :], ACT.Copy, scale=inv),
                               m, after_q)
                    DENSE.free(i, qf)
                    sh = ve.do(lambda e, r=r: e.stream_shuffle(QS[:, r, :], QF[:, r, :], [v ^ 8 for v in range(32)]),
                               qf, after_q)
                    s2 = po.do(lambda e, r=r: e.tensor_tensor(QS[:, r, :], QS[:, r, :], ROPE[:, 1, :], ALU.mult),
                               sh, g_c2.done)
                    c2 = ve.do(lambda e, r=r: e.tensor_tensor(QF[:, r, :], QF[:, r, :], ROPE[:, 0, :], ALU.mult),
                               sh, g_c2.done)
                    ad = ve.do(lambda e, r=r: e.tensor_tensor(QF[:, r, :], QF[:, r, :], QS[:, r, :], ALU.add), s2, c2)
                    hi = ac.do(lambda e, c=c, r=r: e.activation(QP[0][:, c, :], QF[:, r, :], ACT.Copy),
                               ad, free["QP"])
                    lo = po.do(lambda e, c=c, r=r: e.tensor_tensor(QP[1][:, c, :], QF[:, r, :], QP[0][:, c, :],
                                                                  ALU.subtract), hi, free["QP"])
                    Q2.free(r, hi, lo)
                else:
                    hi = ac.do(lambda e, c=c, w=width, bank=bank: e.activation(
                        QP[0][0:w, c, :], bank[0:w, :], ACT.Copy, scale=inv), m, free["QP"])
                    lo = ve.do(lambda e, c=c, w=width, bank=bank: e.scalar_tensor_tensor(
                        QP[1][0:w, c, :], bank[0:w, :], inv, QP[0][0:w, c, :], ALU.mult, ALU.subtract),
                        hi, free["QP"])
                    DENSE.free(i, hi, lo)
                is_q = c < 2
                blocks = ((0, 0), (1, 1), (2, 0)) if is_q else ((0, 0), (1, 0), (2, 1))
                heads = (8 * c if is_q else (8 * (c - 2) if l == 0 else 0), 4 if width == 64 else 8)
                for blk, j in blocks:
                    dst = (SQ if is_q else SK)[16 * blk:16 * blk + 16, heads[0]:heads[0] + heads[1], :]
                    sp.dma(dst, QP[j][0:width, c, :], g_st, (hi, lo)[j], free["SQ" if is_q else "SK"],
                           z_sq, z_k1)
                yield 1300
            stacked = g_st.done
            free["QP"] = [stacked]
            v0 = 2 * D if l == 0 else 320
            vw = 16 * KH
            per = T // vw if vw < T else 1
            per = min(per, NT)
            v_ready = []
            for t0 in range(0, NT, per):
                i, bank, after = DENSE.take()
                for t in range(t0, t0 + per):
                    for s, (jw, jx) in enumerate(TERMS):
                        for k in range(2):
                            m = pe.do(lambda e, t0=t0, jw=jw, jx=jx, k=k, s=s, t=t, bank=bank: e.matmul(
                                bank[:, (t - t0) * vw:(t - t0 + 1) * vw], xt[jx][:, k, t * P:(t + 1) * P],
                                WA[l][:, jw, k, v0:v0 + vw],
                                start=s == 0 and k == 0, stop=s == 2 and k == 1),
                                after, inc=s == 2 and k == 1)
                vv = ac.do(lambda e, per=per, t0=t0, bank=bank: e.activation(
                    V[:, t0:t0 + per, 0:KH, 0:16],
                    bank[:, 0:per * vw].rearrange("p (t h d) -> p t h d", t=per, h=KH), ACT.Copy, scale=inv),
                    m, free["V"])
                DENSE.free(i, vv)
                v_ready.append(vv)
                yield 1300
            XTR.free(n, m)

            def khead(h):
                return h if l == 0 else h % 4

            maxed = {}

            def max_pass(g):
                got = []
                for t in range(NT):
                    per = [4, 2, 1, 1][t]
                    kw = (t + 1) * P
                    for h0 in range(0, 4, per):
                        i, bank, after = MAXB.take()
                        for a in range(per):
                            h = 4 * g + h0 + a
                            pe.do(lambda e, a=a, h=h, t=t, kw=kw, bank=bank: e.matmul(
                                bank[:, a * kw:(a + 1) * kw], SQ[0:96, h, t * P:(t + 1) * P],
                                SK[0:96, khead(h), 0:kw], start=a == 0, stop=False, skip_group_check=True),
                                stacked, consts["alibi"] if l else None, z_k1, after, inc=False)
                        for a in range(per):
                            m = pe.do(lambda e, a=a, t=t, kw=kw, bank=bank: e.matmul(
                                bank[:, a * kw + t * P:(a + 1) * kw], IDH[:, :], MASK[:, 0, :],
                                start=False, stop=True, skip_group_check=True), g_c2.done, inc=a == per - 1)
                        r = ve.do(lambda e, g=g, h0=h0, t=t, per=per, kw=kw, bank=bank: e.tensor_reduce(
                            MX[:, g, h0:h0 + per, t], bank[:, 0:per * kw].rearrange("p (a k) -> p a k", a=per),
                            AX.X, ALU.max, negate=True), m, free["MX"])
                        MAXB.free(i, r)
                        got.append(r)
                        yield 330
                i, bank, after = MAXB.take()
                tr = pe.do(lambda e, bank=bank: e.transpose(bank[0:16, 0:P], MX[:, g, :, :].rearrange("p h t -> p (h t)"),
                                                 ID[:, :]), got, after)
                nm = ac.do(lambda e, bank=bank: e.activation(NM[:, g, :], bank[0:16, 0:P], ACT.Copy), tr, free["NM"])
                MAXB.free(i, nm)
                gr = group(f"g_nm{l}{b}{g}")
                sp.dma(SQ[96:97, 4 * g:4 * g + 4, :].rearrange("o h (t q) -> o (h t) q", t=NT), NM[:, g, :], gr,
                       nm, free["SQM"], z_sq)
                maxed[g] = (gr.done, tr)

            LAYOUT = [(0, 0), (0, 1), (0, 2), (1, 0), (1, 1)]
            exps = {}

            def place(a, kb):
                return [(0, 0), (T, 0), (2 * T, 0), (T + 384, 0)][kb][0] + (
                    0 if a == 0 else (3 * T if kb != 2 else 256))

            def st_pass(g):
                slot, pbuf, after_p = PR.take()
                got = []
                for pr in range(2):
                    h = 4 * g + 2 * pr
                    todo = [[(0, 0)], [(0, 1), (0, 3)], [(0, 2), (1, 2)], [(1, 0)], [(1, 1), (1, 3)]]
                    for s, items in enumerate(todo):
                        i, bank, after = STB.take()
                        at = 0
                        cols = []
                        for a, kb in items:
                            w = T - kb * P
                            pe.do(lambda e, a=a, kb=kb, w=w, at=at, bank=bank, h=h: e.matmul(
                                bank[:, at:at + w], SK[0:QROWS, khead(h + a), kb * P:(kb + 1) * P],
                                SQ[0:QROWS, h + a, kb * P:T], start=at == 0, stop=False, skip_group_check=True),
                                maxed[g][0], after, inc=False)
                            assert place(a, kb) == s * T + at
                            cols.append(at)
                            at += w
                        for at in cols:
                            m = pe.do(lambda e, at=at, bank=bank: e.matmul(
                                bank[:, at:at + P], IDH[:, :], MASK[:, 1, :], start=False, stop=True,
                                skip_group_check=True), inc=at == cols[-1])
                        ex = ac.do(lambda e, pr=pr, s=s, bank=bank, pbuf=pbuf: e.activation(
                            pbuf[:, pr, s * T:(s + 1) * T], bank[:, :], ACT.Exp, scale=0.25), m, after_p)
                        STB.free(i, ex)
                        got.append(ex)
                        yield 330
                exps[g] = (slot, pbuf, got, m)

            outs = []

            def pv_pass(g):
                slot, pbuf, got, _ = exps[g]
                i, bank, after = PVB.take()
                for kb in range(NT):
                    for a in range(4):
                        at = place(a % 2, kb)
                        w = T - kb * P
                        m = pe.do(lambda e, a=a, kb=kb, at=at, w=w: e.matmul(
                            bank[32 * a:32 * a + 32, kb * P:T], V[:, kb, khead(4 * g + a), :],
                            pbuf[:, a // 2, at:at + w], start=kb == 0, stop=kb == NT - 1),
                            got, v_ready, z_v, after, inc=kb == NT - 1 and a == 3)
                    yield 900 - 200 * kb
                PR.free(slot, m)
                o = ac.do(lambda e: e.activation(OT[:, g, :], bank[:, :], ACT.Copy), m, free["OT"])
                PVB.free(i, o)
                outs.append(o)
                return m

            def both(x, y):
                a, bb = x, y
                while True:
                    done = 0
                    for s in (a, bb):
                        try:
                            yield next(s)
                        except StopIteration:
                            done += 1
                    if done == 2:
                        return

            yield from max_pass(0)
            yield from max_pass(1)
            for g in range(4):
                if g + 2 < 4:
                    yield from both(st_pass(g), max_pass(g + 2))
                else:
                    yield from st_pass(g)
                if g >= 1:
                    yield from pv_pass(g - 1)
            last_st = exps[3][3]
            last_pv = yield from pv_pass(3)
            free["MX"] = [maxed[g][1] for g in range(4)]
            free["NM"] = [maxed[g][0] for g in range(4)]
            free["SQ"] = free["SK"] = free["SQM"] = [last_st]
            free["V"] = [last_pv]

            g_dc = group(f"g_dc{l}{b}")
            for a in range(4):
                sp.dma(DC[32 * a:32 * a + 32, :],
                       OT[32 * a + 16:32 * a + 17, :, :].rearrange("o g (s t) -> o (g s) t", t=64),
                       g_dc, outs, free["DC"])
            rc = ve.do(lambda e: e.reciprocal(DC[:, :], DC[:, :]), g_dc.done)
            g_so = group(f"g_so{l}{b}")
            sp.dma(scratch[b % 2], DC[:, :], g_so, rc, free["SCR"])
            stores.append(g_so)
            g_si = group(f"g_si{l}{b}")
            for a in range(4):
                src = scratch[b % 2, 32 * a:32 * a + 32, :].rearrange("(o p) t -> o (p t)", o=1)
                rows = 17 if l == 1 else 16
                sp.dma(RB[32 * a:32 * a + rows, :, :].rearrange("p g t -> p (g t)"),
                       src.to_broadcast([rows, 4 * T]), g_si, g_so.done, free["RB"], zeroed)
            free["DC"] = [g_so.done]
            free["SCR"] = [g_si.done]
            yield 7000
            c_ready = []
            for g in range(4):
                cc = po.do(lambda e, g=g: e.tensor_tensor(OT[:, g, :], OT[:, g, :], RB[:, g, :], ALU.mult),
                           g_si.done, outs)
                hi = ac.do(lambda e, g=g: e.activation(CH[0][:, g, :], OT[:, g, :], ACT.Copy, scale=CS), cc, free["CH"])
                lo = ve.do(lambda e, g=g: e.scalar_tensor_tensor(CH[1][:, g, :], OT[:, g, :], CS, CH[0][:, g, :],
                                                                ALU.mult, ALU.subtract), hi, cc, free["CH"])
                c_ready += [hi, lo]
                yield 300
            free["RB"] = [cc]
            free["OT"] = [hi, lo, g_dc.done]
            new = []
            for pair in range(2):
                i, bank, after = DENSE.take()
                for q in range(2):
                    t = 2 * pair + q
                    steps = [(g, jc, jw) for jc, jw in TERMS for g in range(4)]
                    for s, (g, jc, jw) in enumerate(steps):
                        m = pe.do(lambda e, g=g, jc=jc, jw=jw, t=t, q=q, s=s, bank=bank: e.matmul(
                            bank[:, q * D:(q + 1) * D], CH[jc][:, g, t * P:(t + 1) * P], WO[l][:, jw, g, :],
                            start=s == 0, stop=s == 11), c_ready, w_att[l], after, inc=s == 11)
                xv = X[:, NT * b + 2 * pair:NT * b + 2 * pair + 2, :].rearrange("p t n -> p (t n)")
                y = ve.do(lambda e, xv=xv, bank=bank: e.scalar_tensor_tensor(
                    xv, bank[:, :], 1.0 / (CS * WS), xv, ALU.mult, ALU.add), m, x_read)
                DENSE.free(i, y)
                new.append(y)
                yield 2700
            free["QP"] = [m]
            x_ready[b] = new

        def seq(*gens):
            for g in gens:
                yield from g

        def finish(b):
            g = group(f"g_out{b}")
            sp.dma(out[:, NT * b:NT * b + NT, :], X[:, NT * b:NT * b + NT, :], g, x_ready[b])
            stores.append(g)
            yield 1

        def prepare_a0():
            w_att[0] = attention_weights(0, g_a0.done)
            zeroed.append(po.do(lambda e: e.memset(RB[:, :, :], 0.0), w_att[0]))
            yield 1

        def prepare_l1():
            yield from ternary_weights()
            g = group("g_a1")
            sp.dma(ra[1], wqkv1, g)
            sp.dma(ro[1], wo1, g)
            w_att[1] = attention_weights(1, g.done)
            yield 1

        def begin_l1():
            g = group("g_ali")
            sp.dma(SQ[48:54, :, :], alibi_q, g, free["SQ"])
            sp.dma(SK[48:54, 0:4, :], alibi_k, g, free["SK"])
            consts["alibi"] = g.done
            yield 1

        F, A = 20000.0, 46000.0
        interleave((F, ffn(0, 0)), (F / 8, seq(prepare_a0(), prepare_l1())))
        interleave((A, attention(0, 0)), (F, ffn(1, 0)))
        interleave((A, attention(1, 0)), (3 * F, seq(ffn(2, 0), ffn(0, 0), ffn(0, 1))))
        interleave((A, attention(2, 0)), (3 * F, seq(ffn(3, 0), ffn(1, 0), ffn(1, 1))))
        interleave((A, attention(3, 0)), (2 * F, seq(ffn(2, 0), ffn(2, 1))))
        interleave((1, begin_l1()))
        interleave((A, attention(0, 1)), (2 * F, seq(ffn(3, 0), ffn(3, 1))))
        interleave((A, attention(1, 1)), (F, seq(ffn(0, 1), finish(0))))
        interleave((A, attention(2, 1)), (F, seq(ffn(1, 1), finish(1))))
        interleave((A, attention(3, 1)), (F, seq(ffn(2, 1), finish(2))))
        interleave((F, seq(ffn(3, 1), finish(3))))

        sp.wait([g.done for g in stores])

        block = ctx.enter_context(nc.Block())

        @block.sync
        def _(e):
            sp.replay(e)

        @block.tensor
        def _(e):
            pe.replay(e)

        @block.vector
        def _(e):
            ve.replay(e)

        @block.scalar
        def _(e):
            ac.replay(e)

        @block.gpsimd
        def _(e):
            po.replay(e)


def kernel(**inputs):
    import numpy as np
    import concourse.bacc as bacc
    from concourse.bass_utils import run_bass_kernel_spmd

    a = {k: np.asarray(v) for k, v in inputs.items()}

    def rows(w):
        return np.ascontiguousarray(w.reshape(2, P, -1).transpose(1, 0, 2))

    def hidden(w):
        full = w[:640].reshape(5, P, -1)
        last = np.concatenate([w[640:], w[640:]], 0)[None]
        return np.ascontiguousarray(np.concatenate([full, last], 0).transpose(1, 0, 2))

    p = np.arange(P)
    perm8 = (p & 7) * 16 + ((p >> 3) & 1) * 8 + (p >> 4)
    q4 = np.arange(64)
    perm4 = (q4 & 3) * 16 + (q4 >> 2)
    perm8b = (p & 7) * 16 + (p >> 3)

    def pad_o(w, bias):
        o = np.zeros((4, 4, 32, D), np.float32)
        o[:, :, :16] = w.reshape(4, 4, 16, D)
        if bias is not None:
            o[0, 0, 16] = bias
        return np.ascontiguousarray(o.reshape(4, P, D).transpose(1, 0, 2))

    wq, wk = a["L0_attn_Wq"].T, a["L0_attn_Wk"].T
    qkv0 = np.concatenate([wq[:, perm8], wq[:, P + perm8], wk[:, perm8], wk[:, P + perm8], a["L0_attn_Wv"].T], 1)
    wq, wkv = a["L1_attn_Wq"], a["L1_attn_Wkv"]
    qkv1 = np.concatenate([wq[:, perm8b], wq[:, P + perm8b], wkv[:, perm4], wkv[:, 64:]], 1)

    t = np.arange(T, dtype=np.float32)
    inv_freq = (1.0 / np.float32(10000.0) ** (np.arange(0, 16, 2, dtype=np.float32) / np.float32(16))).astype(np.float32)
    ang = (t[None, :] * inv_freq[p >> 4][:, None]).astype(np.float32)
    sign = np.where((p >> 3) & 1, 1.0, -1.0)[:, None]
    rope = np.stack([np.cos(ang.astype(np.float64)), sign * np.sin(ang.astype(np.float64))], 1).astype(np.float32)

    import ml_dtypes
    qk = np.arange(P)
    m0 = np.where(qk[None, :] > qk[:, None], -1e30, 0.0)
    mask = np.stack([m0, m0.T], 1).astype(ml_dtypes.bfloat16)
    ident = np.eye(P, dtype=np.float32)

    start = 2.0 ** (-2.0 ** (-(np.log2(16) - 3.0)))
    slopes = np.array([start ** (i + 1) for i in range(16)], np.float32).astype(np.float64) * 4.0

    def three(v):
        out = []
        for _ in range(3):
            h = v.astype(np.float16)
            out.append(h)
            v = v - h.astype(np.float64)
        return out

    sl = three(np.broadcast_to(slopes[:, None], (16, T)).astype(np.float64))
    sq = three(-slopes[:, None] * np.arange(T)[None, :])
    alibi_q = np.ascontiguousarray(np.stack(sl + sq, 0))
    kk = np.broadcast_to(np.arange(T).astype(np.float16), (4, T))
    alibi_k = np.ascontiguousarray(np.stack([kk] * 3 + [np.ones((4, T), np.float16)] * 3, 0))

    x = a["L0_attn_hidden_states"].reshape(NB * NT, P, D).transpose(1, 0, 2)
    sgu = np.stack([hidden(a["L0_ffn_s_gate"][:, None])[:, :, 0], hidden(a["L0_ffn_s_up"][:, None])[:, :, 0]], 1)
    arrays = {
        "x_in": x,
        "wqkv0": rows(qkv0),
        "wo0": pad_o(a["L0_attn_Wo"].T, None),
        "gu0": rows(np.concatenate([a["L0_ffn_wq_gate"].T, a["L0_ffn_wq_up"].T], 1)),
        "sgu0": sgu,
        "wd0": hidden(a["L0_ffn_wq_down"].T),
        "sd0": np.broadcast_to(a["L0_ffn_s_down"][None], (P, D)),
        "wqkv1": rows(qkv1),
        "wo1": pad_o(a["L1_attn_Wo"], a["L1_attn_bo"]),
        "gu1": rows(np.concatenate([a["L1_ffn_w1"].T, a["L1_ffn_w2"].T], 1)),
        "wd1": hidden(a["L1_ffn_w3"].T),
        "rope": rope,
        "mask": mask,
        "ident": ident,
        "identh": ident.astype(ml_dtypes.bfloat16),
        "alibi_q": alibi_q,
        "alibi_k": alibi_k,
    }
    arrays = {k: np.ascontiguousarray(v) for k, v in arrays.items()}
    nc = bacc.Bacc("TRN2", target_bir_lowering=False, num_devices=1)
    args = [nc.dram_tensor(k, v.shape, mybir.dt.from_np(v.dtype), kind="ExternalInput").ap() for k, v in arrays.items()]
    scratch = nc.dram_tensor("scratch", (2, P, 64), F32, kind="Internal").ap()
    out = nc.dram_tensor("out", (P, NB * NT, D), F32, kind="ExternalOutput").ap()
    macaron_kernel(nc, *args, scratch, out)
    r = run_bass_kernel_spmd(nc, [arrays], core_ids=[0])
    y = np.asarray(r.results[0]["out"])
    return np.ascontiguousarray(y.transpose(1, 0, 2)).reshape(NB, T, D)
```

```python
import concourse.bass as bass
from concourse import mybir
from contextlib import ExitStack

F32 = mybir.dt.float32
F16 = mybir.dt.float16
BF16 = mybir.dt.bfloat16
I32 = mybir.dt.int32
ACT = mybir.ActivationFunctionType
ALU = mybir.AluOpType
AX = mybir.AxisListType

P = 128
NB = 4
T = 512
NT = 4
D = 256
HID = 704
NH = 16
FC = 6
XS = 16.0
HS = 16.0
WS = 64.0
CS = 16.0
QROWS = 97


HOP = 170.8
DMA_RATE = 360.0
DMA_LATENCY = 1900.0


def latest(tokens):
    t = 0.0
    for x in tokens:
        if isinstance(x, list):
            t = max(t, latest(x))
        elif x is not None:
            t = max(t, x[2] + HOP)
    return t


class Queue:

    def __init__(self, name, sem, base, rate):
        self.name, self.sem, self.count, self.items, self.seen = name, sem, 0, [], {}
        self.base, self.rate, self.t = base, rate, 0.0

    def wait(self, tokens):
        for t in tokens:
            if t is None:
                continue
            if isinstance(t, list):
                self.wait(t)
                continue
            sem, value, _ = t
            if self.seen.get(id(sem), 0) < value:
                self.seen[id(sem)] = value
                self.items.append(lambda e, s=sem, v=value: e.wait_ge(s, v))

    def do(self, fn, *after, inc=True, n=512, f=1.0):
        self.wait(after)
        self.t = max(self.t, latest(after)) + self.base + n * f * self.rate
        if not inc:
            self.items.append(fn)
            return None
        self.count += 1
        self.items.append(lambda e, f=fn: f(e).then_inc(self.sem, 1))
        return (self.sem, self.count, self.t)

    def dma(self, out, in_, group, *after):
        self.wait(after)
        self.t = max(self.t, latest(after)) + 650.0
        group.count += 16
        size = 2 if out.dtype in (F16, BF16) else 4
        for r in out.shape:
            size *= r
        Queue.wire = max(Queue.wire, self.t) + size / DMA_RATE
        group.t = max(group.t, Queue.wire + DMA_LATENCY)
        self.items.append(lambda e, s=group.sem: e.dma_start(out, in_).then_inc(s, 16))

    wire = 0.0

    def replay(self, e):
        for f in self.items:
            f(e)


class Group:

    def __init__(self, sem):
        self.sem, self.count, self.t = sem, 0, 0.0

    @property
    def done(self):
        return (self.sem, self.count, self.t)


class Ring:

    def __init__(self, bufs):
        self.bufs = bufs
        self.idle = [(i, []) for i in range(len(bufs))]

    def take(self):
        i, after = self.idle.pop(0)
        return i, self.bufs[i], after

    def free(self, i, *tokens):
        self.idle.append((i, list(tokens)))


def interleave(clock, streams):
    SLACK, BEHIND, AHEAD = 108.4, 1478.7, 1480.9
    spent = {n: 0.0 for n in streams}
    share = {n: w for n, (w, _) in streams.items()}
    live = {n: g for n, (_, g) in streams.items()}
    needs = {n: ([], None) for n in streams}
    blocked = set()
    now, idle = 0.0, 0

    def start(n):
        tokens, ring = needs[n]
        t = latest(tokens)
        if ring is not None and ring.idle:
            t = max(t, latest(ring.idle[0][1]))
        return max(t, clock.t + SLACK)

    while live:
        ready = [n for n in live if n not in blocked]
        if not ready:
            idle += 1
            assert idle < 4, "every stream waits for another"
            blocked.clear()
            continue
        n = min(ready, key=lambda m: (start(m), spent[m]))
        now = max(now, spent[n])
        try:
            step = next(live[n])
        except StopIteration:
            del live[n]
            blocked.clear()
            continue
        if step is None:
            blocked.add(n)
            spent[n] = max(spent[n], now - BEHIND)
            continue
        idle = 0
        blocked.clear()
        cost, tokens, ring = step
        needs[n] = (tokens, ring)
        spent[n] = max(spent[n], now - AHEAD) + cost / share[n]


def macaron_kernel(nc, x_in, wqkv0, wo0, gu0, sgu0, wd0, sd0, wqkv1, wo1, gu1, wd1,
                   rope, mask, ident, identh, alibi_q, alibi_k, scratch, out):
    ctx = ExitStack()
    with ctx:
        def sb(name, shape, dt=F32):
            return ctx.enter_context(nc.sbuf_tensor(name, shape, dt))

        def sem(name):
            return ctx.enter_context(nc.semaphore(name))

        X = sb("X", [P, NB * NT, D])
        WGU = [sb(f"WGU{l}", [P, 2, 2 * HID], F16) for l in range(2)]
        WD = [sb(f"WD{l}", [P, FC, D], F16) for l in range(2)]
        SGU = sb("SGU", [P, 2, FC])
        SGH = sb("SGH", [P, FC])
        SUH = sb("SUH", [P, FC])
        SD = sb("SD", [P, D])
        NQKV = [768, 384]
        WA = [sb(f"WA{l}", [P, 2, 2, NQKV[l]], F16) for l in range(2)]
        WO = [sb(f"WO{l}", [P, 2, 4, D], F16) for l in range(2)]
        ROPE = sb("ROPE", [P, 2, T])
        MASK = sb("MASK", [P, 2, P], BF16)
        ID = sb("ID", [P, P])
        IDH = sb("IDH", [P, P], BF16)
        LN = [[sb(f"XN{i}", [P, NT, D]), sb(f"ST{i}", [P, NT, 6]), sb(f"MV{i}", [P, NT, 2]),
               sb(f"VE{i}", [P, NT]), sb(f"YR{i}", [P, NT]), sb(f"AR{i}", [P, NT])] for i in range(2)]
        XT = [[sb(f"XT{i}{j}", [P, 2, T], F16) for j in range(2)] for i in range(2)]
        TH = sb("TH", [P, 3, T])
        HH = [sb(f"HH{j}", [P, FC * T - 256], F16) for j in range(2)]
        QF = sb("QF", [P, 2, T])
        QS = sb("QS", [P, 2, T])
        ONE = QS[:, 0, 0:P]
        QPB = sb("QPB", [P, 2, 2, T], F16)
        CH = [sb(f"CH{j}", [P, 4, T], F16) for j in range(2)]
        SQ = sb("SQ", [QROWS, NH, T], F16)
        SK = sb("SK", [QROWS, NH, T], F16)
        V = sb("V", [P, NT, NH, 32])
        MX = sb("MX", [P, 4, 4, NT])
        NM = sb("NM", [16, 4, P], F16)
        PB = [sb(f"PB{i}", [P, 2, 5 * T]) for i in range(2)]
        OT = sb("OT", [P, 4, T])
        DC = sb("DC", [P, 64])
        RB = sb("RB", [P, 4, T])
        GA = sb("GA", [P, 3, 22])
        GS = sb("GS", [P, 6])
        TB = CH[1][:, :, :].rearrange("p c t -> p (c t)")

        banks = [ctx.enter_context(nc.psum_tensor(f"B{i}", [P, T], F32)) for i in range(8)]
        DENSE = Ring(banks[0:3])
        MAXB = Ring(banks[3:5])
        STB = Ring(banks[5:7])
        PVB = Ring(banks[7:8])

        pe = Queue("pe", sem("s_pe"), 2.0, 1 / 2.4)
        ve = Queue("ve", sem("s_ve"), 65.0, 1 / 0.96)
        ac = Queue("ac", sem("s_ac"), 50.0, 1 / 1.2)
        po = Queue("po", sem("s_po"), 40.0, 2.1)
        sp = Queue("sp", None, 0.0, 0.0)
        stores = []

        def group(name):
            return Group(sem(name))

        g_const = group("g_const")
        sp.dma(X[:, 0:NT, :], x_in[:, 0:NT, :], g_const)
        sp.dma(ID[:, :], ident, g_const)
        g_w0 = [group(f"g_w0{k}") for k in range(3)]
        raw = [PB[l][:, :, :].rearrange("p a n -> p (a n)") for l in range(2)]
        rawi = raw[0][:, 0:4 * HID + FC * D].bitcast(I32)
        rgu = raw[1][:, 0:4 * HID].rearrange("p (k n) -> p k n", k=2)
        rd = raw[1][:, 4 * HID:4 * HID + FC * D].rearrange("p (c n) -> p c n", c=FC)
        rgui = rawi[:, 0:4 * HID].rearrange("p (k n) -> p k n", k=2)
        rdi = rawi[:, 4 * HID:].rearrange("p (c n) -> p c n", c=FC)
        for k in range(2):
            sp.dma(rgui[:, k, :], gu0[:, k, :], g_w0[k])
        g_s0 = group("g_s0")
        sp.dma(SGU[:, :, :], sgu0, g_s0)
        sp.dma(SD[:, :], sd0, g_s0)
        sp.dma(rdi, wd0, g_w0[2])
        g_x = group("g_x")
        sp.dma(X[:, NT:, :], x_in[:, NT:, :], g_x)
        g_a0 = group("g_a0")
        ra = [OT[:, 0:3, :].rearrange("p g t -> p (g t)").rearrange("p (k n) -> p k n", k=2),
              raw[0][:, 4 * HID + FC * D:].rearrange("p (k n) -> p k n", k=2)]
        ro = [RB[:, 0:2, :].rearrange("p g t -> p (g t)").rearrange("p (c n) -> p c n", c=4),
              CH[0][:, :, :].rearrange("p c t -> p (c t)").bitcast(F32).rearrange("p (c n) -> p c n", c=4)]
        sp.dma(ra[0], wqkv0, g_a0)
        sp.dma(ro[0], wo0, g_a0)
        g_c2 = group("g_c2")
        sp.dma(ROPE[:, :, :], rope, g_c2)
        sp.dma(MASK[:, :, :], mask, g_c2)
        sp.dma(IDH[:, :], identh, g_c2)

        z_sq = po.do(lambda e: e.memset(SQ[:, :, :], 0.0))
        z_sk = po.do(lambda e: e.memset(SK[:, :, :], 0.0))
        z_k1 = po.do(lambda e: e.memset(SK[96:97, :, :], 1.0), z_sk)
        z_v = po.do(lambda e: e.memset(V[:, :, :, 16:32], 1.0), z_k1)
        z_one = po.do(lambda e: e.memset(ONE, 1.0))

        w_gu0 = [ac.do(lambda e, k=k: e.activation(WGU[0][:, k, :], rgui[:, k, :], ACT.Copy, bias=-128.0),
                       g_w0[k].done, n=1408) for k in range(2)]
        w_d0 = ac.do(lambda e: e.activation(WD[0][:, :, :], rdi, ACT.Copy, bias=-128.0), g_w0[2].done, n=1536)
        w_ffn = [[w_gu0, w_d0], None]

        def attention_weights(l, loaded):
            n = NQKV[l]
            up = ac.do(lambda e: e.activation(ra[l], ra[l], ACT.Copy, scale=WS), loaded, n=2 * n)
            hi = ac.do(lambda e: e.activation(WA[l][:, 0, :, :], ra[l], ACT.Copy), up, n=2 * n)
            lo = po.do(lambda e: e.tensor_tensor(WA[l][:, 1, :, :], ra[l], WA[l][:, 0, :, :], ALU.subtract),
                       up, hi, n=2 * n)
            oup = ac.do(lambda e: e.activation(ro[l], ro[l], ACT.Copy, scale=WS), n=1024)
            ohi = ac.do(lambda e: e.activation(WO[l][:, 0, :, :], ro[l], ACT.Copy), oup, n=1024)
            olo = po.do(lambda e: e.tensor_tensor(WO[l][:, 1, :, :], ro[l], WO[l][:, 0, :, :], ALU.subtract),
                        oup, ohi, n=1024)
            return [hi, lo, ohi, olo]

        w_att = [None, None]
        zeroed, one_read = [], []

        def ternary_weights():
            g = group("g_w1")
            sp.dma(rgu, gu1, g)
            sp.dma(rd, wd1, g)
            yield 100, [g.done], None
            for i in range(2):
                a = ve.do(lambda e, i=i: e.tensor_reduce(
                    GA[:, i, :].rearrange("p (k a) -> p k a", k=2),
                    rgu[:, :, i * HID:(i + 1) * HID].rearrange("p k (a b) -> p k a b", b=64),
                    AX.X, ALU.add, apply_absolute_value=True), g.done, n=1408)
            yield 300, [g.done], None
            b = ve.do(lambda e: e.tensor_reduce(GA[:, 2, 0:20], rd[:, 0:5, :].rearrange("p c (a b) -> p (c a) b", b=64),
                                                AX.X, ALU.add, apply_absolute_value=True), n=1280)
            c = ve.do(lambda e: e.tensor_reduce(GA[:, 2, 20:21], rd[0:P, 5:6, :], AX.XY, ALU.add,
                                                apply_absolute_value=True))
            c2 = ve.do(lambda e: e.tensor_scalar(GA[:, 2, 21:22], GA[:, 2, 20:21], -0.5, None, ALU.mult), c)
            d = ve.do(lambda e: e.tensor_reduce(GS[:, 0:3], GA[:, :, :], AX.X, ALU.add), a, b, c2)
            yield 300, [d], DENSE
            i, bank, after = DENSE.take()
            m = pe.do(lambda e: e.matmul(bank[:, 0:3], ONE, GS[:, 0:3], start=True, stop=True), d, z_one, after)
            th = ve.do(lambda e: e.tensor_scalar(GS[:, 0:3], bank[:, 0:3], 1.0 / (HID * D), 1e-8, ALU.mult, ALU.add), m, n=4)
            one_read.append(m)
            DENSE.free(i, th)
            t5 = ve.do(lambda e: e.tensor_scalar(GS[:, 3:6], GS[:, 0:3], -0.5, None, ALU.mult), th, n=4)
            t6 = ve.do(lambda e: e.tensor_scalar(GS[:, 0:3], GS[:, 0:3], 0.5, None, ALU.mult), t5, n=4)
            yield 300, [], None
            last, got = None, []
            for k in range(2):
                u = []
                for i in range(2):
                    u.append(ve.do(lambda e, k=k, i=i: e.tensor_scalar(
                        TB[:, i * HID:(i + 1) * HID], rgu[:, k, i * HID:(i + 1) * HID],
                        GS[:, 3 + i:4 + i], None, ALU.is_lt), t6, last))
                for i in range(2):
                    last = ve.do(lambda e, k=k, i=i: e.scalar_tensor_tensor(
                        WGU[1][:, k, i * HID:(i + 1) * HID], rgu[:, k, i * HID:(i + 1) * HID], GS[:, i:i + 1],
                        TB[:, i * HID:(i + 1) * HID], ALU.is_gt, ALU.subtract), u)
                got.append(last)
                yield 300, [], None
            for k in range(2):
                src = rd[:, 3 * k:3 * k + 3, :].rearrange("p c n -> p (c n)")
                u = ve.do(lambda e, s=src: e.tensor_scalar(TB[:, 0:768], s, GS[:, 5:6], None, ALU.is_lt), last)
                last = ve.do(lambda e, s=src, k=k: e.scalar_tensor_tensor(
                    WD[1][:, 3 * k:3 * k + 3, :].rearrange("p c n -> p (c n)"), s, GS[:, 2:3], TB[:, 0:768],
                    ALU.is_gt, ALU.subtract), u)
                got.append(last)
            w_ffn[1] = got
            yield 300, [], None

        XTR = Ring(XT)
        x_ready = [[g_const.done]] + [[g_const.done, g_x.done] for _ in range(3)]
        LNR = Ring(LN)

        def normalise(b, fine=False):
            yield 0, [x_ready[b]], None
            while not LNR.idle:
                yield None
            slot, (XN, ST6, MV, VE, YR, AR), after_ln = LNR.take()
            st = [ve.do(lambda e, i=i: e.bn_stats(ST6[:, i, :], X[:, NT * b + i, :]), x_ready[b], after_ln, n=256)
                  for i in range(NT)]
            yield 0, [], None
            if fine:
                p1 = ve.do(lambda e: e.tensor_reduce(
                    XN[:, 0, 0:64], X[:, NT * b:NT * b + NT, :].rearrange("p t (a c) -> p (t a) c", c=16),
                    AX.X, ALU.add), x_ready[b], after_ln, n=1024)
                yield 0, [p1], None
            mv = [ve.do(lambda e, i=i: e.bn_aggr(MV[:, i, :], ST6[:, i, :]), st[i], n=10) for i in range(NT)]
            if fine:
                p2 = ve.do(lambda e: e.tensor_reduce(
                    XN[:, 1, 0:NT], XN[:, 0, 0:64].rearrange("p (t a) -> p t a", t=NT), AX.X, ALU.add), p1, after_ln, n=64)
            yield 0, [mv], None
            q = ve.do(lambda e: e.tensor_scalar(VE[:, :], MV[:, :, 1], 1e-5, 1.0 / (XS * XS), ALU.add, ALU.mult), mv, n=4)
            if fine:
                mv.append(ve.do(lambda e: e.tensor_scalar(MV[:, :, 0], XN[:, 1, 0:NT], 1.0 / D, None, ALU.mult),
                                p2, mv, n=4))
            yield 0, [q], None
            s = ve.do(lambda e: e.tensor_scalar(AR[:, :].bitcast(I32), VE[:, :].bitcast(I32), 1, None,
                                                ALU.logical_shift_right), q, n=4)
            yield 0, [s], None
            y = ve.do(lambda e: e.tensor_scalar(YR[:, :].bitcast(I32), AR[:, :].bitcast(I32), -1.0, 1597463007.0,
                                                ALU.mult, ALU.add), s, n=4)
            yield 0, [y], None
            for _ in range(3):
                a = ve.do(lambda e: e.scalar_tensor_tensor(AR[:, :], YR[:, :], -0.5, YR[:, :], ALU.mult, ALU.mult), y, n=4)
                yield 0, [a], None
                a = ve.do(lambda e: e.tensor_tensor(AR[:, :], AR[:, :], VE[:, :], ALU.mult), a, n=4)
                yield 0, [a], None
                y = ve.do(lambda e: e.scalar_tensor_tensor(YR[:, :], AR[:, :], 1.5, YR[:, :], ALU.add, ALU.mult), a, n=4)
                yield 0, [y], None
            xn = []
            for i in range(NT):
                xn.append(ve.do(lambda e, i=i: e.tensor_scalar(XN[:, i, :], X[:, NT * b + i, :], MV[:, i, 0:1],
                                                               YR[:, i:i + 1], ALU.subtract, ALU.mult), y, mv, n=256))
                yield 0, [], None
            return slot, XN, xn

        def turn(normal):
            slot, XN, xn = normal
            yield 0, [xn], DENSE
            while not XTR.idle:
                yield None
            n, xt, after_xt = XTR.take()
            his, trs, held = [], [], []
            for k in range(2):
                i, bank, after = DENSE.take()
                for t in range(NT):
                    tr = pe.do(lambda e, k=k, t=t, bank=bank: e.transpose(
                        bank[:, t * P:(t + 1) * P], XN[:, t, k * P:(k + 1) * P], ID[:, :]),
                        xn[t], g_const.done, after, inc=t == NT - 1, n=256)
                trs.append(tr)
                his.append(ac.do(lambda e, k=k, bank=bank: e.activation(xt[0][:, k, :], bank[:, :], ACT.Copy),
                                 tr, after_xt))
                held.append((i, bank))
            parts = list(his)
            for k, (i, bank) in enumerate(held):
                lo = ve.do(lambda e, k=k, bank=bank: e.tensor_tensor(xt[1][:, k, :], bank[:, :], xt[0][:, k, :],
                                                                    ALU.subtract), his[k], after_xt)
                DENSE.free(i, his[k], lo)
                parts.append(lo)
            LNR.free(slot, trs, xn[-1])
            yield 880, [parts], DENSE
            return n, xt, parts, xn

        H2 = Ring([0, 1, 2])
        ffn_free = {"HH": []}

        def ffn(b, l):
            while len(w_ffn[0]) < 4 or (b, l) not in normals or not normals[b, l]:
                yield None
            n, xt, x_parts, x_read = yield from turn(normals[b, l].pop())
            ready, late = [], []

            def split(c, r, w, h):
                hi = ac.do(lambda e: e.activation(HH[0][:, c * T:c * T + w], TH[:, r, 0:w], ACT.Copy), h, ffn_free["HH"], n=w)
                lo = po.do(lambda e: e.tensor_tensor(HH[1][:, c * T:c * T + w], TH[:, r, 0:w], HH[0][:, c * T:c * T + w],
                                                     ALU.subtract), hi, h, n=w)
                H2.free(r, lo, hi)
                ready.extend([hi, lo])

            for c in range(FC):
                half = c == FC - 1
                w = T // 2 if half else T
                got = []
                for u in range(2):
                    i, bank, after = DENSE.take()
                    for j in range(2):
                        for k in range(2):
                            col = u * HID + c * P
                            first, last = j == 0 and k == 0, j == 1 and k == 1
                            if half:
                                for z in range(2):
                                    m = pe.do(lambda e, z=z, j=j, k=k, col=col, bank=bank, first=first, last=last:
                                              e.matmul(bank[64 * z:64 * z + 64, 0:256], WGU[l][:, k, col:col + 64],
                                                       xt[j][:, k, 256 * z:256 * z + 256], start=first, stop=last),
                                              x_parts, w_ffn[l], after, inc=last and z == 1, n=140)
                            else:
                                m = pe.do(lambda e, j=j, k=k, col=col, bank=bank, first=first, last=last:
                                          e.matmul(bank[:, :], WGU[l][:, k, col:col + P], xt[j][:, k, :],
                                                   start=first, stop=last),
                                          x_parts, w_ffn[l], after, inc=last)
                    got.append((i, bank, m))
                (ig, bg, mg), (iu, bu, mu) = got
                r, _, after_h = H2.take()
                if l == 0:
                    th = ac.do(lambda e, c=c, r=r, bg=bg, w=w: e.activation(TH[:, r, 0:w], bg[:, 0:w], ACT.Tanh,
                                                                            scale=SGH[:, c:c + 1]), mg, after_h, n=w)
                    t1 = ve.do(lambda e, r=r, bg=bg, w=w: e.scalar_tensor_tensor(
                        TH[:, r, 0:w], TH[:, r, 0:w], 1.0, bg[:, 0:w], ALU.add, ALU.mult), th, mg, after_h, n=w)
                    h = ve.do(lambda e, c=c, r=r, bu=bu, w=w: e.scalar_tensor_tensor(
                        TH[:, r, 0:w], bu[:, 0:w], SUH[:, c:c + 1], TH[:, r, 0:w], ALU.mult, ALU.mult), mu, t1, n=w)
                    DENSE.free(ig, th, t1)
                else:
                    th = ac.do(lambda e, r=r, bg=bg, w=w: e.activation(TH[:, r, 0:w], bg[:, 0:w], ACT.Tanh,
                                                                       scale=0.5 / XS), mg, after_h, n=w)
                    h = ve.do(lambda e, r=r, bu=bu, w=w: e.scalar_tensor_tensor(
                        TH[:, r, 0:w], TH[:, r, 0:w], 1.0, bu[:, 0:w], ALU.add, ALU.mult), th, mu, after_h, n=w)
                    DENSE.free(ig, th)
                DENSE.free(iu, h)
                if late:
                    split(*late.pop())
                late.append((c, r, w, h))
                yield 1740 / (2 if half else 1), [], DENSE
            XTR.free(n, mu)
            yield 0, [h], None
            split(*late.pop())
            yield 0, [ready], DENSE
            new = []
            for pair in range(2):
                i, bank, after = DENSE.take()
                for q in range(2):
                    t = 2 * pair + q
                    z = t // 2
                    steps = [(c, j) for c in range(FC) for j in range(2)]
                    for s, (c, j) in enumerate(steps):
                        if c < FC - 1:
                            lhs, rhs = HH[j][:, c * T + t * P:c * T + (t + 1) * P], WD[l][:, c, :]
                        else:
                            lhs = HH[j][64 * z:64 * z + 64, c * T + (t % 2) * P:c * T + (t % 2 + 1) * P]
                            rhs = WD[l][64 * z:64 * z + 64, c, :]
                        m = pe.do(lambda e, lhs=lhs, rhs=rhs, bank=bank, q=q, s=s:
                                  e.matmul(bank[:, q * D:(q + 1) * D], lhs, rhs, start=s == 0, stop=s == 11),
                                  ready, w_ffn[l], after, inc=s == 11, n=256)
                xv = X[:, NT * b + 2 * pair:NT * b + 2 * pair + 2, :].rearrange("p t n -> p (t n)")
                if l == 0:
                    r, _, after_d = H2.take()
                    sdb = SD[:, :].unsqueeze(1).to_broadcast([P, 2, D])
                    d = ve.do(lambda e, r=r, bank=bank, sdb=sdb: e.scalar_tensor_tensor(
                        TH[:, r, :].rearrange("p (t n) -> p t n", t=2), bank[:, :].rearrange("p (t n) -> p t n", t=2),
                        0.5 / HS, sdb, ALU.mult, ALU.mult), m, after_d)
                    DENSE.free(i, d)
                    y = po.do(lambda e, r=r, xv=xv: e.tensor_tensor(xv, xv, TH[:, r, :], ALU.add), d, x_read)
                    H2.free(r, y)
                else:
                    y = ve.do(lambda e, xv=xv, bank=bank: e.scalar_tensor_tensor(
                        xv, bank[:, :], 0.25 / XS, xv, ALU.mult, ALU.add), m, x_read)
                    DENSE.free(i, y)
                new.append(y)
                yield 2600, [ready], DENSE
            ffn_free["HH"] = [m]
            x_ready[b] = new

        Q2 = Ring([0, 1])
        QPR = Ring([0, 1])
        PR = Ring(PB)
        TERMS = [(0, 0), (0, 1), (1, 0)]
        inv = 1.0 / (XS * WS)
        ATT = [(b, l) for l in range(2) for b in range(NB)]
        fronts, valued, cores, tails, quads_done = set(), set(), set(), set(), set()
        att = [{} for _ in ATT]
        free = {"SQ": [[] for _ in range(4)], "SK": [[] for _ in range(4)], "V": [], "MX": [[]] * 4, "NM": [[]] * 4,
                "OT": [[]] * 4, "DC": [], "RB": [], "CH": [], "SCR": [[], []]}

        def khead(n, h):
            return h if n < NB else 4 * (n - NB) + h % 4

        def front(n):
            b, l = ATT[n]
            slot, xt, x_parts, x_read = yield from turn((yield from normalise(b)))
            stacked = att[n]["stacked"] = {}
            att[n].update(slot=slot, xt=xt, x_read=x_read, x_parts=x_parts)
            order = (0, 2, 1, 3) if l == 0 else (2, 0, 1)
            for c in order:
                width = 64 if (l == 1 and c == 2) else P
                i, bank, after = DENSE.take()
                for s, (jw, jx) in enumerate(TERMS):
                    for k in range(2):
                        m = pe.do(lambda e, c=c, jw=jw, jx=jx, k=k, s=s, width=width, bank=bank: e.matmul(
                            bank[0:width, :], WA[l][:, jw, k, c * P:c * P + width], xt[jx][:, k, :],
                            start=s == 0 and k == 0, stop=s == 2 and k == 1),
                            x_parts, w_att[l], after, inc=s == 2 and k == 1)
                rq, _, after_p = QPR.take()
                QP = [QPB[:, rq, j, :] for j in range(2)]
                if l == 0:
                    r, _, after_q = Q2.take()
                    qf = ac.do(lambda e, r=r, bank=bank: e.activation(QF[:, r, :], bank[:, :], ACT.Copy, scale=inv),
                               m, after_q)
                    DENSE.free(i, qf)
                    yield 0, [qf], None
                    sh = ve.do(lambda e, r=r: e.stream_shuffle(QS[:, r, :], QF[:, r, :], [v ^ 8 for v in range(32)]),
                               qf, after_q)
                    s2 = po.do(lambda e, r=r: e.tensor_tensor(QS[:, r, :], QS[:, r, :], ROPE[:, 1, :], ALU.mult),
                               sh, g_c2.done)
                    c2 = ve.do(lambda e, r=r: e.tensor_tensor(QF[:, r, :], QF[:, r, :], ROPE[:, 0, :], ALU.mult),
                               sh, g_c2.done)
                    yield 1300, [s2, c2], None
                    ad = ve.do(lambda e, r=r: e.tensor_tensor(QF[:, r, :], QF[:, r, :], QS[:, r, :], ALU.add), s2, c2)
                    yield 0, [ad], None
                    hi = ac.do(lambda e, r=r, QP=QP: e.activation(QP[0], QF[:, r, :], ACT.Copy), ad, after_p)
                    lo = po.do(lambda e, r=r, QP=QP: e.tensor_tensor(QP[1], QF[:, r, :], QP[0], ALU.subtract),
                               hi, after_p)
                    Q2.free(r, hi, lo)
                else:
                    hi = ac.do(lambda e, width=width, bank=bank, QP=QP: e.activation(
                        QP[0][0:width], bank[0:width, :], ACT.Copy, scale=inv), m, after_p)
                    lo = ve.do(lambda e, width=width, bank=bank, QP=QP: e.scalar_tensor_tensor(
                        QP[1][0:width], bank[0:width, :], inv, QP[0][0:width], ALU.mult, ALU.subtract),
                        hi, after_p)
                    DENSE.free(i, hi, lo)
                is_q = c < 2
                h0 = 8 * (c % 2) if (is_q or l == 0) else 4 * (n - NB)
                nh = 4 if width == 64 else 8
                need = (n - 1 if width == P else NB - 1, (h0 + nh) // 4 - 1)
                while n and need not in quads_done:
                    yield None
                g = group(f"g_st{n}{c}")
                was = free["SQ" if is_q else "SK"]
                before = [was[h0 // 4], was[(h0 + nh - 1) // 4]]
                for blk, j in (((0, 0), (1, 1), (2, 0)) if is_q else ((0, 0), (1, 0), (2, 1))):
                    dst = (SQ if is_q else SK)[16 * blk:16 * blk + 16, h0:h0 + nh, :]
                    sp.dma(dst, QP[j][0:width], g, (hi, lo)[j], before, z_sq, z_k1)
                QPR.free(rq, g.done)
                stacked[c] = g.done
                fronts.add((n, c))
                yield 0 if l == 0 else 1300, [x_parts], DENSE
            fronts.add((n, "all"))

        def values(n):
            b, l = ATT[n]
            xt = att[n]["xt"]
            KH = NH if l == 0 else 4
            v0 = 2 * D if l == 0 else 320
            vw = 16 * KH
            per = min(T // vw, NT)
            got = []
            for t0 in range(0, NT, per):
                i, bank, after = DENSE.take()
                for t in range(t0, t0 + per):
                    for s, (jw, jx) in enumerate(TERMS):
                        for k in range(2):
                            m = pe.do(lambda e, jw=jw, jx=jx, k=k, s=s, t=t, t0=t0, bank=bank: e.matmul(
                                bank[:, (t - t0) * vw:(t - t0 + 1) * vw], xt[jx][:, k, t * P:(t + 1) * P],
                                WA[l][:, jw, k, v0:v0 + vw],
                                start=s == 0 and k == 0, stop=s == 2 and k == 1),
                                att[n]["x_parts"], w_att[l], after, inc=s == 2 and k == 1, n=vw)
                vv = ac.do(lambda e, t0=t0, bank=bank: e.activation(
                    V[:, t0:t0 + per, 0:KH, 0:16],
                    bank[:, 0:per * vw].rearrange("p (t h d) -> p t h d", t=per, h=KH), ACT.Copy, scale=inv),
                    m, free["V"], z_v)
                DENSE.free(i, vv)
                got.append(vv)
                yield 1300, [], DENSE
            XTR.free(att[n]["slot"], m)
            att[n]["v"] = got
            valued.add(n)

        def max_pass(n, g):
            b, l = ATT[n]
            got = []
            stacked = [att[n]["stacked"][c] for c in (g // 2, 2 + g // 2 if l == 0 else 2)]
            for t in range(NT):
                per = [4, 2, 1, 1][t]
                kw = (t + 1) * P
                for h0 in range(0, 4, per):
                    i, bank, after = MAXB.take()
                    for a in range(per):
                        h = 4 * g + h0 + a
                        pe.do(lambda e, a=a, h=h, t=t, kw=kw, bank=bank: e.matmul(
                            bank[:, a * kw:(a + 1) * kw], SQ[0:96, h, t * P:(t + 1) * P],
                            SK[0:96, khead(n, h), 0:kw], start=a == 0, stop=False, skip_group_check=True),
                            stacked, [alibi[g], alibi[n - NB]] if l else None, z_k1, after, inc=False, n=kw)
                    for a in range(per):
                        m = pe.do(lambda e, a=a, t=t, kw=kw, bank=bank: e.matmul(
                            bank[:, a * kw + t * P:(a + 1) * kw], IDH[:, :], MASK[:, 0, :],
                            start=False, stop=True, skip_group_check=True), g_c2.done, inc=a == per - 1, n=P)
                    r = ve.do(lambda e, h0=h0, t=t, per=per, kw=kw, bank=bank: e.tensor_reduce(
                        MX[:, g, h0:h0 + per, t], bank[:, 0:per * kw].rearrange("p (a k) -> p a k", a=per),
                        AX.X, ALU.max, negate=True), m, free["MX"][g], n=per * kw)
                    MAXB.free(i, r)
                    got.append(r)
                    yield 330, [stacked], MAXB
            yield 0, [got], MAXB
            i, bank, after = MAXB.take()
            tr = pe.do(lambda e, bank=bank: e.transpose(bank[0:16, 0:P], MX[:, g, :, :].rearrange("p h t -> p (h t)"),
                                             ID[:, :]), got, after, n=256)
            nm = ac.do(lambda e, bank=bank: e.activation(NM[:, g, :], bank[0:16, 0:P], ACT.Copy), tr, free["NM"][g], n=P)
            MAXB.free(i, nm)
            gr = group(f"g_nm{n}{g}")
            ac.dma(SQ[96:97, 4 * g:4 * g + 4, :].rearrange("o h (t q) -> o (h t) q", t=NT), NM[:, g, :], gr,
                   nm, free["SQ"][g], z_sq)
            free["MX"][g] = [tr]
            free["NM"][g] = [gr.done]
            att[n]["max", g] = gr.done

        PLACE = {(0, 0): 0, (0, 1): T, (0, 3): T + 384, (0, 2): 2 * T, (1, 2): 2 * T + 256,
                 (1, 0): 3 * T, (1, 1): 4 * T, (1, 3): 4 * T + 384}

        def st_pass(n, g):
            b, l = ATT[n]
            slot, pbuf, after_p = PR.take()
            got = []
            wants = att[n]["max", g]
            yield 0, [wants, after_p], STB
            for pr in range(2):
                h = 4 * g + 2 * pr
                todo = [[(0, 0)], [(0, 1), (0, 3)], [(0, 2), (1, 2)], [(1, 0)], [(1, 1), (1, 3)]]
                for s, items in enumerate(todo):
                    i, bank, after = STB.take()
                    for a, kb in items:
                        w = T - kb * P
                        at = PLACE[a, kb] - s * T
                        pe.do(lambda e, a=a, kb=kb, w=w, at=at, bank=bank, h=h: e.matmul(
                            bank[:, at:at + w], SK[0:QROWS, khead(n, h + a), kb * P:(kb + 1) * P],
                            SQ[0:QROWS, h + a, kb * P:T], start=at == 0, stop=False, skip_group_check=True),
                            wants, after, inc=False, n=w)
                    for a, kb in items:
                        at = PLACE[a, kb] - s * T
                        m = pe.do(lambda e, at=at, bank=bank: e.matmul(
                            bank[:, at:at + P], IDH[:, :], MASK[:, 1, :], start=False, stop=True,
                            skip_group_check=True), inc=(a, kb) == items[-1], n=P)
                    ex = ac.do(lambda e, pr=pr, s=s, bank=bank, pbuf=pbuf: e.activation(
                        pbuf[:, pr, s * T:(s + 1) * T], bank[:, :], ACT.Exp, scale=0.25), m, after_p)
                    STB.free(i, ex)
                    got.append(ex)
                    yield 330, [], STB
            free["SQ"][g] = [m]
            free["SK"][g] = [m]
            if n == NB - 1:
                ga = group(f"g_ali{g}")
                sp.dma(SQ[48:54, 4 * g:4 * g + 4, :], alibi_q[:, 4 * g:4 * g + 4, :], ga, m)
                sp.dma(SK[48:54, 4 * g:4 * g + 4, :], alibi_k, ga, m)
                alibi.append(ga.done)
            quads_done.add((n, g))
            att[n]["exp", g] = (slot, pbuf, got)

        def pv_pass(n, g):
            b, l = ATT[n]
            slot, pbuf, got = att[n]["exp", g]
            yield 0, [got, att[n]["v"]], PVB
            i, bank, after = PVB.take()
            for kb in range(NT):
                for a in range(4):
                    at = PLACE[a % 2, kb]
                    w = T - kb * P
                    m = pe.do(lambda e, a=a, kb=kb, at=at, w=w: e.matmul(
                        bank[32 * a:32 * a + 32, kb * P:T], V[:, kb, 4 * g + a if l == 0 else a, :],
                        pbuf[:, a // 2, at:at + w], start=kb == 0, stop=kb == NT - 1),
                        got, att[n]["v"], z_v, after, inc=kb == NT - 1 and a == 3, n=w)
                yield 900 - 200 * kb, [], None
            PR.free(slot, m)
            o = ac.do(lambda e: e.activation(OT[:, g, :], bank[:, :], ACT.Copy), m, free["OT"][g])
            PVB.free(i, o)
            att[n]["o", g] = o
            if g == 3:
                free["V"] = [m]

        def max_stream():
            for n in range(len(ATT)):
                l = ATT[n][1]
                for g in range(4):
                    while any((n, c) not in fronts for c in (g // 2, 2 + g // 2 if l == 0 else 2)):
                        yield None
                    while n and (n - 1, g) not in quads_done:
                        yield None
                    yield from max_pass(n, g)

        def st_stream():
            for n in range(len(ATT)):
                for g in range(4):
                    while ("max", g) not in att[n] or not PR.idle:
                        yield None
                    yield from st_pass(n, g)

        def pv_stream():
            for n in range(len(ATT)):
                while (n, "all") not in fronts:
                    yield None
                yield from values(n)
                for g in range(4):
                    while (n, g) not in quads_done or (n and n - 1 not in tails):
                        yield None
                    yield from pv_pass(n, g)
                cores.add(n)

        def tail(n):
            b, l = ATT[n]
            while n not in cores:
                yield None
            outs = [att[n]["o", g] for g in range(4)]
            yield 0, [outs], None
            g_dc = group(f"g_dc{n}")
            sp.dma(DC[:, :], OT[16:P:32, :, :].rearrange("a g (s t) -> a (g s) t", t=64), g_dc, outs, free["DC"])
            yield 0, [g_dc.done], None
            rc = ve.do(lambda e: e.reciprocal(DC[:, :], DC[:, :]), g_dc.done)
            g_so = group(f"g_so{n}")
            sp.dma(scratch[n % 2], DC[:, :], g_so, rc, free["SCR"][n % 2])
            stores.append(g_so)
            g_si = group(f"g_si{n}")
            src = scratch[n % 2].rearrange("(a o p) t -> a o (p t)", a=4, o=1)
            sp.dma(RB[:, :, :].rearrange("p g t -> p (g t)"), src.to_broadcast([4, 32, 4 * T]), g_si,
                   g_so.done, free["RB"], zeroed)
            free["DC"] = [g_so.done]
            free["SCR"][n % 2] = [g_si.done]
            yield 0, [g_si.done], None
            c_ready = []
            ccs = [po.do(lambda e, g=g: e.tensor_tensor(OT[:, g, :], OT[:, g, :], RB[:, g, :], ALU.mult),
                         g_si.done, outs) for g in range(4)]
            for g, cc in enumerate(ccs):
                yield 0, [cc], None
                hi = ac.do(lambda e, g=g: e.activation(CH[0][:, g, :], OT[:, g, :], ACT.Copy, scale=CS), cc, free["CH"])
                lo = ve.do(lambda e, g=g: e.scalar_tensor_tensor(CH[1][:, g, :], OT[:, g, :], CS, CH[0][:, g, :],
                                                                ALU.mult, ALU.subtract), hi, cc, free["CH"])
                c_ready += [hi, lo]
                free["OT"][g] = [hi, lo, g_dc.done]
            yield 0, [c_ready], DENSE
            free["RB"] = [cc]
            tails.add(n)
            new = []
            for pair in range(2):
                i, bank, after = DENSE.take()
                for q in range(2):
                    t = 2 * pair + q
                    steps = [(g, jc, jw) for jc, jw in TERMS for g in range(4)]
                    for s, (g, jc, jw) in enumerate(steps):
                        m = pe.do(lambda e, g=g, jc=jc, jw=jw, t=t, q=q, s=s, bank=bank: e.matmul(
                            bank[:, q * D:(q + 1) * D], CH[jc][:, g, t * P:(t + 1) * P], WO[l][:, jw, g, :],
                            start=s == 0, stop=s == 11), c_ready, w_att[l], after, inc=s == 11, n=256)
                xv = X[:, NT * b + 2 * pair:NT * b + 2 * pair + 2, :].rearrange("p t n -> p (t n)")
                y = ve.do(lambda e, xv=xv, bank=bank: e.scalar_tensor_tensor(
                    xv, bank[:, :], 1.0 / (CS * WS), xv, ALU.mult, ALU.add), m, att[n]["x_read"])
                DENSE.free(i, y)
                new.append(y)
                yield 2600, [], DENSE
            free["CH"] = [m]
            x_ready[b] = new
            state[b] = ("A", l)

        alibi, prepared, normals, ffns_done = [], set(), {}, []
        state = {}

        def fronts_stream():
            for n, (b, l) in enumerate(ATT):
                while not prepared or state.get(b) != ("F", l) or (n and n - 1 not in valued):
                    yield None
                yield from front(n)

        FFNS = [(b, 0, None, ("F", 0)) for b in range(NB)]
        for b in range(NB):
            FFNS += [(b, 0, ("A", 0), ("M", 0)), (b, 1, ("M", 0), ("F", 1))]
        FFNS += [(b, 1, ("A", 1), ("E", 1)) for b in range(NB)]

        def norms_stream():
            for b, l, before, _ in FFNS:
                while state.get(b) != before or any(normals.values()):
                    yield None
                normals[b, l] = [(yield from normalise(b, l == 0))]

        def ffn_stream(first, end):
            while len(ffns_done) < first:
                yield None
            for b, l, before, says in FFNS[first:end]:
                yield from ffn(b, l)
                state[b] = says
                ffns_done.append((b, l))
                if says == ("E", 1):
                    g = group(f"g_out{b}")
                    sp.dma(out[:, NT * b:NT * b + NT, :], X[:, NT * b:NT * b + NT, :], g, x_ready[b])
                    stores.append(g)

        def tails_stream():
            for n in range(len(ATT)):
                yield from tail(n)

        def prepare():
            yield 100, [g_s0.done], None
            w_sg = ve.do(lambda e: e.tensor_scalar(SGH[:, :], SGU[:, 0, :], 0.5 / XS, None, ALU.mult), g_s0.done, n=6)
            w_su = ve.do(lambda e: e.scalar_tensor_tensor(SUH[:, :], SGU[:, 0, :], 0.5 * HS / (XS * XS),
                                                          SGU[:, 1, :], ALU.mult, ALU.mult), n=6)
            w_ffn[0] += [w_sg, w_su]
            yield 100, [g_a0.done], None
            w_att[0] = attention_weights(0, g_a0.done)
            zeroed.append(po.do(lambda e: e.memset(RB[:, :, :], 0.0), w_att[0], n=1024))
            yield 100, [], None
            yield from ternary_weights()
            g = group("g_a1")
            sp.dma(ra[1], wqkv1, g)
            sp.dma(ro[1], wo1, g)
            yield 100, [g.done], None
            w_att[1] = attention_weights(1, g.done)
            read = [w_ffn[1], w_att[0], w_att[1], one_read]
            PR.idle = [(i, read) for i in range(2)]
            Q2.idle = [(i, read) for i in range(2)]
            free["OT"] = [read] * 4
            free["RB"] = free["CH"] = read
            prepared.add(0)

        interleave(pe, {"st": (1.5511, st_stream()), "max": (0.0971, max_stream()), "pv": (0.1084, pv_stream()),
                    "front": (0.3447, fronts_stream()), "tail": (0.5426, tails_stream()), "norm": (0.3499, norms_stream()), "ffn": (0.2660, ffn_stream(0, 12)),
                    "last": (0.0161, ffn_stream(12, 16)),
                    "prepare": (0.1308, prepare())})

        sp.wait([g.done for g in stores])

        block = ctx.enter_context(nc.Block())

        @block.sync
        def _(e):
            sp.replay(e)

        @block.tensor
        def _(e):
            pe.replay(e)

        @block.vector
        def _(e):
            ve.replay(e)

        @block.scalar
        def _(e):
            ac.replay(e)

        @block.gpsimd
        def _(e):
            po.replay(e)


def kernel(**inputs):
    import numpy as np
    import concourse.bacc as bacc
    from concourse.bass_utils import run_bass_kernel_spmd

    a = {k: np.asarray(v) for k, v in inputs.items()}

    def rows(w):
        return np.ascontiguousarray(w.reshape(2, P, -1).transpose(1, 0, 2))

    def hidden(w):
        full = w[:640].reshape(5, P, -1)
        last = np.concatenate([w[640:], w[640:]], 0)[None]
        return np.ascontiguousarray(np.concatenate([full, last], 0).transpose(1, 0, 2))

    p = np.arange(P)
    perm8 = (p & 7) * 16 + ((p >> 3) & 1) * 8 + (p >> 4)
    q4 = np.arange(64)
    perm4 = (q4 & 3) * 16 + (q4 >> 2)
    perm8b = (p & 7) * 16 + (p >> 3)

    def pad_o(w, bias):
        o = np.zeros((4, 4, 32, D), np.float32)
        o[:, :, :16] = w.reshape(4, 4, 16, D)
        if bias is not None:
            o[0, 0, 16] = bias
        return np.ascontiguousarray(o.reshape(4, P, D).transpose(1, 0, 2))

    wq, wk = a["L0_attn_Wq"].T, a["L0_attn_Wk"].T
    qkv0 = np.concatenate([wq[:, perm8], wq[:, P + perm8], wk[:, perm8], wk[:, P + perm8], a["L0_attn_Wv"].T], 1)
    wq, wkv = a["L1_attn_Wq"], a["L1_attn_Wkv"]
    qkv1 = np.concatenate([wq[:, perm8b], wq[:, P + perm8b], wkv[:, perm4], wkv[:, 64:]], 1)

    t = np.arange(T, dtype=np.float32)
    inv_freq = (1.0 / np.float32(10000.0) ** (np.arange(0, 16, 2, dtype=np.float32) / np.float32(16))).astype(np.float32)
    ang = (t[None, :] * inv_freq[p >> 4][:, None]).astype(np.float32)
    sign = np.where((p >> 3) & 1, 1.0, -1.0)[:, None]
    rope = np.stack([np.cos(ang.astype(np.float64)), sign * np.sin(ang.astype(np.float64))], 1).astype(np.float32)

    import ml_dtypes
    qk = np.arange(P)
    m0 = np.where(qk[None, :] > qk[:, None], -1e30, 0.0)
    mask = np.stack([m0, m0.T], 1).astype(ml_dtypes.bfloat16)
    ident = np.eye(P, dtype=np.float32)

    start = 2.0 ** (-2.0 ** (-(np.log2(16) - 3.0)))
    slopes = np.array([start ** (i + 1) for i in range(16)], np.float32).astype(np.float64) * 4.0

    def three(v):
        out = []
        for _ in range(3):
            h = v.astype(np.float16)
            out.append(h)
            v = v - h.astype(np.float64)
        return out

    sl = three(np.broadcast_to(slopes[:, None], (16, T)).astype(np.float64))
    sq = three(-slopes[:, None] * np.arange(T)[None, :])
    alibi_q = np.ascontiguousarray(np.stack(sl + sq, 0))
    kk = np.broadcast_to(np.arange(T).astype(np.float16), (4, T))
    alibi_k = np.ascontiguousarray(np.stack([kk] * 3 + [np.ones((4, T), np.float16)] * 3, 0))

    x = a["L0_attn_hidden_states"].reshape(NB * NT, P, D).transpose(1, 0, 2)
    sgu = np.stack([hidden(a["L0_ffn_s_gate"][:, None])[:, :, 0], hidden(a["L0_ffn_s_up"][:, None])[:, :, 0]], 1)
    arrays = {
        "x_in": x,
        "wqkv0": rows(qkv0),
        "wo0": pad_o(a["L0_attn_Wo"].T, None),
        "gu0": rows(np.concatenate([a["L0_ffn_wq_gate"].T, a["L0_ffn_wq_up"].T], 1)),
        "sgu0": sgu,
        "wd0": hidden(a["L0_ffn_wq_down"].T),
        "sd0": np.broadcast_to(a["L0_ffn_s_down"][None], (P, D)),
        "wqkv1": rows(qkv1),
        "wo1": pad_o(a["L1_attn_Wo"], a["L1_attn_bo"]),
        "gu1": rows(np.concatenate([a["L1_ffn_w1"].T, a["L1_ffn_w2"].T], 1)),
        "wd1": hidden(a["L1_ffn_w3"].T),
        "rope": rope,
        "mask": mask,
        "ident": ident,
        "identh": ident.astype(ml_dtypes.bfloat16),
        "alibi_q": alibi_q,
        "alibi_k": alibi_k,
    }
    arrays = {k: np.ascontiguousarray(v) for k, v in arrays.items()}
    nc = bacc.Bacc("TRN2", target_bir_lowering=False, num_devices=1)
    args = [nc.dram_tensor(k, v.shape, mybir.dt.from_np(v.dtype), kind="ExternalInput").ap() for k, v in arrays.items()]
    scratch = nc.dram_tensor("scratch", (2, P, 64), F32, kind="Internal").ap()
    out = nc.dram_tensor("out", (P, NB * NT, D), F32, kind="ExternalOutput").ap()
    macaron_kernel(nc, *args, scratch, out)
    r = run_bass_kernel_spmd(nc, [arrays], core_ids=[0])
    y = np.asarray(r.results[0]["out"])
    return np.ascontiguousarray(y.transpose(1, 0, 2)).reshape(NB, T, D)
```

```python
import concourse.bass as bass
from concourse import mybir
from contextlib import ExitStack

F32 = mybir.dt.float32
F16 = mybir.dt.float16
BF16 = mybir.dt.bfloat16
I32 = mybir.dt.int32
ACT = mybir.ActivationFunctionType
ALU = mybir.AluOpType
AX = mybir.AxisListType

P = 128
NB = 4
T = 512
NT = 4
D = 256
HID = 704
NH = 16
FC = 6
XS = 16.0
HS = 16.0
WS = 64.0
CS = 16.0
QROWS = 97


HOP = 196.0
DMA_RATE = 360.0
DMA_LATENCY = 1900.0


def latest(tokens):
    t = 0.0
    for x in tokens:
        if isinstance(x, list):
            t = max(t, latest(x))
        elif x is not None:
            t = max(t, x[2] + HOP)
    return t


class Queue:

    def __init__(self, name, sem, base, rate):
        self.name, self.sem, self.count, self.items, self.seen = name, sem, 0, [], {}
        self.base, self.rate, self.t = base, rate, 0.0

    def wait(self, tokens):
        for t in tokens:
            if t is None:
                continue
            if isinstance(t, list):
                self.wait(t)
                continue
            sem, value, _ = t
            if self.seen.get(id(sem), 0) < value:
                self.seen[id(sem)] = value
                self.items.append(lambda e, s=sem, v=value: e.wait_ge(s, v))

    def expect(self, *tokens):
        self.t = max(self.t, latest(tokens))

    def do(self, fn, *after, inc=True, n=512, f=1.0):
        self.wait(after)
        self.t = max(self.t, latest(after)) + self.base + n * f * self.rate
        if not inc:
            self.items.append(fn)
            return None
        self.count += 1
        self.items.append(lambda e, f=fn: f(e).then_inc(self.sem, 1))
        return (self.sem, self.count, self.t)

    def dma(self, out, in_, group, *after):
        self.wait(after)
        self.t = max(self.t, latest(after)) + 650.0
        group.count += 16
        size = 2 if out.dtype in (F16, BF16) else 4
        for r in out.shape:
            size *= r
        Queue.wire = max(Queue.wire, self.t) + size / DMA_RATE
        group.t = max(group.t, Queue.wire + DMA_LATENCY)
        self.items.append(lambda e, s=group.sem: e.dma_start(out, in_).then_inc(s, 16))

    wire = 0.0

    def replay(self, e):
        for f in self.items:
            f(e)


class Group:

    def __init__(self, sem):
        self.sem, self.count, self.t = sem, 0, 0.0

    @property
    def done(self):
        return (self.sem, self.count, self.t)


class Ring:

    def __init__(self, bufs):
        self.bufs = bufs
        self.idle = [(i, []) for i in range(len(bufs))]

    def take(self):
        i, after = self.idle.pop(0)
        return i, self.bufs[i], after

    def free(self, i, *tokens):
        self.idle.append((i, list(tokens)))


def interleave(clock, phase, streams):
    LOOK = {'norm': 1160.0, 'tail': 98.0, 'front': 65.0, 'prepare': 279.0, 'ffn': 74.0}
    SLACK, BEHIND, AHEAD = 184.0, 1311.0, 1514.0
    spent = {n: 0.0 for n in streams}
    share = {n: w for n, (w, _) in streams.items()}
    live = {n: g for n, (_, g) in streams.items()}
    needs = {n: ([], None) for n in streams}
    blocked = set()
    now, idle = 0.0, 0

    def start(n):
        tokens, ring = needs[n]
        t = latest(tokens)
        if ring is not None and ring.idle:
            t = max(t, latest(ring.idle[0][1]))
        return max(t - LOOK.get(n, 0.0), clock.t + SLACK)

    while live:
        ready = [n for n in live if n not in blocked]
        if not ready:
            idle += 1
            assert idle < 4, "every stream waits for another"
            blocked.clear()
            continue
        n = min(ready, key=lambda m: (start(m), spent[m]))
        now = max(now, spent[n])
        try:
            step = next(live[n])
        except StopIteration:
            del live[n]
            blocked.clear()
            continue
        if step is None:
            blocked.add(n)
            spent[n] = max(spent[n], now - BEHIND)
            continue
        idle = 0
        blocked.clear()
        cost, tokens, ring = step
        needs[n] = (tokens, ring)
        spent[n] = max(spent[n], now - AHEAD) + cost / share[n][phase()]


def macaron_kernel(nc, x_in, wqkv0, wo0, gu0, sgu0, wd0, sd0, wqkv1, wo1, gu1, wd1,
                   rope, mask, ident, identh, alibi_q, alibi_k, bo1, scratch, out):
    ctx = ExitStack()
    with ctx:
        def sb(name, shape, dt=F32):
            return ctx.enter_context(nc.sbuf_tensor(name, shape, dt))

        def sem(name):
            return ctx.enter_context(nc.semaphore(name))

        X = sb("X", [P, NB * NT, D])
        WGU = [sb(f"WGU{l}", [P, 2, 2 * HID], F16) for l in range(2)]
        WD = [sb(f"WD{l}", [P, FC, D], F16) for l in range(2)]
        SGU = sb("SGU", [P, 2, FC])
        SGH = sb("SGH", [P, FC])
        SUH = sb("SUH", [P, FC])
        SD = sb("SD", [P, D])
        NQKV = [768, 384]
        WA = [sb(f"WA{l}", [P, 2, 2, NQKV[l]], F16) for l in range(2)]
        WO = [sb(f"WO{l}", [P, 2, 2, D], F16) for l in range(2)]
        BO = sb("BO", [P, D])
        ROPE = sb("ROPE", [P, 2, T])
        MASK = sb("MASK", [P, 2, P], BF16)
        ID = sb("ID", [P, P])
        IDH = sb("IDH", [P, P], BF16)
        LN = [[sb(f"XN{i}", [P, NT, D]), sb(f"ST{i}", [P, NT, 6]), sb(f"MV{i}", [P, NT, 2]),
               sb(f"VE{i}", [P, NT]), sb(f"YR{i}", [P, NT]), sb(f"AR{i}", [P, NT])] for i in range(2)]
        XT = [[sb(f"XT{i}{j}", [P, 2, T], F16) for j in range(2)] for i in range(2)]
        TH = sb("TH", [P, 4, T])
        HX = sb("HX", [P, 2, T // 2], F16)
        HH = [sb(f"HH{j}", [P, FC * T - 256], F16) for j in range(2)]
        QF = sb("QF", [P, 2, T])
        QS = sb("QS", [P, 2, T])
        ONE = sb("ONE", [P, P])
        QPB = sb("QPB", [P, 2, 2, T], F16)
        CH = [sb(f"CH{j}", [P, 2, T], F16) for j in range(2)]
        SQ = sb("SQ", [QROWS, NH, T], F16)
        SK = sb("SK", [QROWS, NH, T], F16)
        V = sb("V", [P, NT, NH, 32])
        MX = sb("MX", [P, 4, 4, NT])
        NM = sb("NM", [16, 4, P], F16)
        PB = [sb(f"PB{i}", [P, 2, 5 * T]) for i in range(2)]
        OT = sb("OT", [P, 4, T])
        DC = sb("DC", [P, 64])
        OC = sb("OC", [P, 2, T])
        RB = sb("RB", [P, 2, T])
        GA = sb("GA", [P, 3, 22])
        GS = sb("GS", [P, 6])
        TB = sb("TB", [P, 2 * HID], F16)

        banks = [ctx.enter_context(nc.psum_tensor(f"B{i}", [P, T], F32)) for i in range(8)]
        DENSE = Ring(banks[0:3])
        MAXB = Ring(banks[3:5])
        STB = Ring(banks[5:7])
        PVB = Ring(banks[7:8])

        pe = Queue("pe", sem("s_pe"), 2.0, 1 / 2.4)
        ve = Queue("ve", sem("s_ve"), 65.0, 1 / 0.96)
        ac = Queue("ac", sem("s_ac"), 50.0, 1 / 1.2)
        po = Queue("po", sem("s_po"), 40.0, 2.1)
        sp = Queue("sp", None, 0.0, 0.0)
        stores = []

        groups = {}

        def group(name):
            if name not in groups:
                groups[name] = Group(sem(name))
            return groups[name]

        g_const = group("g_const")
        sp.dma(X[:, 0:NT, :], x_in[:, 0:NT, :], g_const)
        sp.dma(ID[:, :], ident, g_const)
        g_w0 = [group(f"g_w0{k}") for k in range(3)]
        raw = [PB[l][:, :, :].rearrange("p a n -> p (a n)") for l in range(2)]
        rawi = raw[0][:, 0:4 * HID + FC * D].bitcast(I32)
        rgu = raw[1][:, 0:4 * HID].rearrange("p (k n) -> p k n", k=2)
        rd = raw[1][:, 4 * HID:4 * HID + FC * D].rearrange("p (c n) -> p c n", c=FC)
        rgui = rawi[:, 0:4 * HID].rearrange("p (k n) -> p k n", k=2)
        rdi = rawi[:, 4 * HID:].rearrange("p (c n) -> p c n", c=FC)
        for k in range(2):
            sp.dma(rgui[:, k, :], gu0[:, k, :], g_w0[k])
        g_x1 = group("g_x1")
        sp.dma(X[:, NT:2 * NT, :], x_in[:, NT:2 * NT, :], g_x1)
        g_s0 = group("g_s0")
        sp.dma(SGU[:, :, :], sgu0, g_s0)
        sp.dma(SD[:, :], sd0, g_s0)
        sp.dma(rdi, wd0, g_w0[2])
        g_x = group("g_x")
        sp.dma(X[:, 2 * NT:, :], x_in[:, 2 * NT:, :], g_x)
        g_a0 = group("g_a0")
        ra = [OT[:, 0:3, :].rearrange("p g t -> p (g t)").rearrange("p (k n) -> p k n", k=2),
              raw[0][:, 4 * HID + FC * D:].rearrange("p (k n) -> p k n", k=2)]
        ro = [RB[:, l, :].rearrange("p (c n) -> p c n", c=2) for l in range(2)]
        sp.dma(ra[0], wqkv0, g_a0)
        sp.dma(ro[0], wo0, g_a0)
        sp.dma(BO[:, :], bo1, g_a0)
        g_c2 = group("g_c2")
        sp.dma(ROPE[:, :, :], rope, g_c2)
        sp.dma(MASK[:, :, :], mask, g_c2)
        sp.dma(IDH[:, :], identh, g_c2)

        z_sq = po.do(lambda e: e.memset(SQ[:, :, :], 0.0))
        z_sk = po.do(lambda e: e.memset(SK[:, :, :], 0.0))
        z_k1 = po.do(lambda e: e.memset(SK[96:97, :, :], 1.0), z_sk)
        z_v = po.do(lambda e: e.memset(V[:, :, :, 16:32], 1.0), z_k1)
        z_one = po.do(lambda e: e.memset(ONE[:, :], 1.0))

        w_gu0 = [ac.do(lambda e, k=k: e.activation(WGU[0][:, k, :], rgui[:, k, :], ACT.Copy, bias=-128.0),
                       g_w0[k].done, n=1408) for k in range(2)]
        w_d0 = ac.do(lambda e: e.activation(WD[0][:, :, :], rdi, ACT.Copy, bias=-128.0), g_w0[2].done, n=1536)
        w_ffn = [[w_gu0, w_d0], None]

        def attention_weights(l, loaded):
            n = NQKV[l]
            up = ac.do(lambda e: e.activation(ra[l], ra[l], ACT.Copy, scale=WS), loaded, n=2 * n)
            hi = ac.do(lambda e: e.activation(WA[l][:, 0, :, :], ra[l], ACT.Copy), up, n=2 * n)
            lo = po.do(lambda e: e.tensor_tensor(WA[l][:, 1, :, :], ra[l], WA[l][:, 0, :, :], ALU.subtract),
                       up, hi, n=2 * n)
            oup = ac.do(lambda e: e.activation(ro[l], ro[l], ACT.Copy, scale=WS), n=512)
            ohi = ac.do(lambda e: e.activation(WO[l][:, 0, :, :], ro[l], ACT.Copy), oup, n=512)
            olo = po.do(lambda e: e.tensor_tensor(WO[l][:, 1, :, :], ro[l], WO[l][:, 0, :, :], ALU.subtract),
                        oup, ohi, n=512)
            return [hi, lo, ohi, olo]

        w_att = [None, None]

        def ternary_weights():
            g = group("g_w1")
            sp.dma(rgu, gu1, g)
            sp.dma(rd, wd1, g)
            yield 100, [g.done], None
            sums = []
            for k in range(2):
                for i in range(2):
                    sums.append(ve.do(lambda e, i=i, k=k: e.tensor_reduce(
                        GA[:, i, 11 * k:11 * k + 11], rgu[:, k, i * HID:(i + 1) * HID].rearrange("p (a b) -> p a b", b=64),
                        AX.X, ALU.add, apply_absolute_value=True), g.done, n=704))
                    yield 300, [], None
            for u in range(2):
                c0, c1 = (0, 3) if u == 0 else (3, 5)
                sums.append(ve.do(lambda e, c0=c0, c1=c1: e.tensor_reduce(
                    GA[:, 2, 4 * c0:4 * c1], rd[:, c0:c1, :].rearrange("p c (a b) -> p (c a) b", b=64),
                    AX.X, ALU.add, apply_absolute_value=True), g.done, n=256 * (c1 - c0)))
                yield 300, [], None
            c = ve.do(lambda e: e.tensor_reduce(GA[:, 2, 20:21], rd[0:P, 5:6, :], AX.XY, ALU.add,
                                                apply_absolute_value=True), n=256)
            c2 = ve.do(lambda e: e.tensor_scalar(GA[:, 2, 21:22], GA[:, 2, 20:21], -0.5, None, ALU.mult), c)
            d = ve.do(lambda e: e.tensor_reduce(GS[:, 0:3], GA[:, :, :], AX.X, ALU.add), sums, c2, n=66)
            yield 300, [d], DENSE
            i, bank, after = DENSE.take()
            m = pe.do(lambda e: e.matmul(bank[:, 0:3], ONE[:, :], GS[:, 0:3], start=True, stop=True), d, z_one, after)
            th = ve.do(lambda e: e.tensor_scalar(GS[:, 0:3], bank[:, 0:3], 1.0 / (HID * D), 1e-8, ALU.mult, ALU.add), m, n=4)
            DENSE.free(i, th)
            t5 = ve.do(lambda e: e.tensor_scalar(GS[:, 3:6], GS[:, 0:3], -0.5, None, ALU.mult), th, n=4)
            t6 = ve.do(lambda e: e.tensor_scalar(GS[:, 0:3], GS[:, 0:3], 0.5, None, ALU.mult), t5, n=4)
            yield 300, [], None
            last, got = None, []
            for k in range(2):
                u = []
                for i in range(2):
                    u.append(ve.do(lambda e, k=k, i=i: e.tensor_scalar(
                        TB[:, i * HID:(i + 1) * HID], rgu[:, k, i * HID:(i + 1) * HID],
                        GS[:, 3 + i:4 + i], None, ALU.is_lt), t6, last, n=400))
                    yield 150, [], None
                for i in range(2):
                    last = ve.do(lambda e, k=k, i=i: e.scalar_tensor_tensor(
                        WGU[1][:, k, i * HID:(i + 1) * HID], rgu[:, k, i * HID:(i + 1) * HID], GS[:, i:i + 1],
                        TB[:, i * HID:(i + 1) * HID], ALU.is_gt, ALU.subtract), u, n=760)
                    yield 150, [], None
                got.append(last)
                yield 300, [], None
            for k in range(2):
                src = rd[:, 3 * k:3 * k + 3, :].rearrange("p c n -> p (c n)")
                u = ve.do(lambda e, s=src: e.tensor_scalar(TB[:, 0:768], s, GS[:, 5:6], None, ALU.is_lt), last, n=430)
                yield 150, [], None
                last = ve.do(lambda e, s=src, k=k: e.scalar_tensor_tensor(
                    WD[1][:, 3 * k:3 * k + 3, :].rearrange("p c n -> p (c n)"), s, GS[:, 2:3], TB[:, 0:768],
                    ALU.is_gt, ALU.subtract), u, n=830)
                yield 150, [], None
                got.append(last)
            w_ffn[1] = got
            yield 300, [], None

        XTR = Ring(XT)
        x_ready = [[g_const.done] * 2, [g_x1.done] * 2, [g_x.done] * 2, [g_x.done] * 2]
        LNR = Ring(LN)

        def normalise(b, fine=False):
            yield 0, [x_ready[b]], None
            while not LNR.idle:
                yield None
            slot, (XN, ST6, MV, VE, YR, AR), after_ln = LNR.take()
            ready = x_ready[b]
            st = [ve.do(lambda e, i=i: e.bn_stats(ST6[:, i, :], X[:, NT * b + i, :]),
                        ready[i // 2] if len(ready) == 2 else ready, after_ln, n=256) for i in range(NT)]
            yield 0, [], None
            if fine:
                p1 = ve.do(lambda e: e.tensor_reduce(
                    XN[:, 0, 0:64], X[:, NT * b:NT * b + NT, :].rearrange("p t (a c) -> p (t a) c", c=16),
                    AX.X, ALU.add), x_ready[b], after_ln, n=1024)
                yield 0, [p1], None
            mv = [ve.do(lambda e, i=i: e.bn_aggr(MV[:, i, :], ST6[:, i, :]), st[i], n=10) for i in range(NT)]
            if fine:
                p2 = ve.do(lambda e: e.tensor_reduce(
                    XN[:, 1, 0:NT], XN[:, 0, 0:64].rearrange("p (t a) -> p t a", t=NT), AX.X, ALU.add), p1, after_ln, n=64)
            yield 0, [mv], None
            q = ve.do(lambda e: e.tensor_scalar(VE[:, :], MV[:, :, 1], 1e-5, 1.0 / (XS * XS), ALU.add, ALU.mult), mv, n=4)
            if fine:
                mv.append(ve.do(lambda e: e.tensor_scalar(MV[:, :, 0], XN[:, 1, 0:NT], 1.0 / D, None, ALU.mult),
                                p2, mv, n=4))
            yield 0, [q], None
            s = ve.do(lambda e: e.tensor_scalar(AR[:, :].bitcast(I32), VE[:, :].bitcast(I32), 1, None,
                                                ALU.logical_shift_right), q, n=4)
            yield 0, [s], None
            y = ve.do(lambda e: e.tensor_scalar(YR[:, :].bitcast(I32), AR[:, :].bitcast(I32), -1.0, 1597463007.0,
                                                ALU.mult, ALU.add), s, n=4)
            yield 0, [y], None
            for _ in range(3):
                a = ve.do(lambda e: e.scalar_tensor_tensor(AR[:, :], YR[:, :], -0.5, YR[:, :], ALU.mult, ALU.mult), y, n=4)
                yield 0, [a], None
                a = ve.do(lambda e: e.tensor_tensor(AR[:, :], AR[:, :], VE[:, :], ALU.mult), a, n=4)
                yield 0, [a], None
                y = ve.do(lambda e: e.scalar_tensor_tensor(YR[:, :], AR[:, :], 1.5, YR[:, :], ALU.add, ALU.mult), a, n=4)
                yield 0, [y], None
            xn = []
            for i in range(NT):
                xn.append(ve.do(lambda e, i=i: e.tensor_scalar(XN[:, i, :], X[:, NT * b + i, :], MV[:, i, 0:1],
                                                               YR[:, i:i + 1], ALU.subtract, ALU.mult), y, mv, n=256))
                yield 0, [], None
            return slot, XN, xn

        def turn(normal):
            slot, XN, xn = normal
            yield 0, [xn], DENSE
            while not XTR.idle:
                yield None
            n, xt, after_xt = XTR.take()
            his, trs, held = [], [], []
            for k in range(2):
                i, bank, after = DENSE.take()
                for t in range(NT):
                    tr = pe.do(lambda e, k=k, t=t, bank=bank: e.transpose(
                        bank[:, t * P:(t + 1) * P], XN[:, t, k * P:(k + 1) * P], ID[:, :]),
                        xn[t], g_const.done, after, inc=t == NT - 1, n=256)
                trs.append(tr)
                his.append(ac.do(lambda e, k=k, bank=bank: e.activation(xt[0][:, k, :], bank[:, :], ACT.Copy),
                                 tr, after_xt))
                held.append((i, bank))
            parts = list(his)
            for k, (i, bank) in enumerate(held):
                lo = ve.do(lambda e, k=k, bank=bank: e.tensor_tensor(xt[1][:, k, :], bank[:, :], xt[0][:, k, :],
                                                                    ALU.subtract), his[k], after_xt)
                DENSE.free(i, his[k], lo)
                parts.append(lo)
            LNR.free(slot, trs, xn[-1])
            yield 880, [parts], DENSE
            return n, xt, parts, xn

        H2 = Ring([0, 1, 2, 3])
        ffn_free = {"HH": []}

        def ffn(b, l):
            while len(w_ffn[0]) < 4 or (b, l) not in normals or not normals[b, l]:
                yield None
            n, xt, x_parts, x_read = yield from turn(normals[b, l].pop())
            ready, late = {}, []

            def split(c, r, w, h):
                hi = ac.do(lambda e: e.activation(HH[0][:, c * T:c * T + w], TH[:, r, 0:w], ACT.Copy), h, ffn_free["HH"], n=w)
                lo = po.do(lambda e: e.tensor_tensor(HH[1][:, c * T:c * T + w], TH[:, r, 0:w], HH[0][:, c * T:c * T + w],
                                                     ALU.subtract), hi, h, n=w)
                H2.free(r, lo, hi)
                if c < FC - 1:
                    ready[c] = [hi, lo]
                    return
                g = group("g_hx")
                for j in range(2):
                    for z in range(2):
                        sp.dma(HX[64 * j:64 * j + 64, z, :], HH[j][64 * z:64 * z + 64, c * T:c * T + w], g,
                               (hi, lo)[j], ffn_free["HH"])
                ready[c] = [g.done]

            for c in (FC - 1, *range(FC - 1)):
                half = c == FC - 1
                w = T // 2 if half else T
                got = []
                for u in range(2):
                    i, bank, after = DENSE.take()
                    pe.expect(x_parts)
                    for j in range(2):
                        for k in range(2):
                            col = u * HID + c * P
                            first, last = j == 0 and k == 0, j == 1 and k == 1
                            if half:
                                for z in range(2):
                                    m = pe.do(lambda e, z=z, j=j, k=k, col=col, bank=bank, first=first, last=last:
                                              e.matmul(bank[64 * z:64 * z + 64, 0:256], WGU[l][:, k, col:col + 64],
                                                       xt[j][:, k, 256 * z:256 * z + 256], start=first, stop=last),
                                              x_parts[2 * j + k], w_ffn[l], after, inc=last and z == 1, n=140)
                            else:
                                m = pe.do(lambda e, j=j, k=k, col=col, bank=bank, first=first, last=last:
                                          e.matmul(bank[:, :], WGU[l][:, k, col:col + P], xt[j][:, k, :],
                                                   start=first, stop=last),
                                          x_parts[2 * j + k], w_ffn[l], after, inc=last)
                    got.append((i, bank, m))
                (ig, bg, mg), (iu, bu, mu) = got
                r, _, after_h = H2.take()
                if l == 0:
                    th = ac.do(lambda e, c=c, r=r, bg=bg, w=w: e.activation(TH[:, r, 0:w], bg[:, 0:w], ACT.Tanh,
                                                                            scale=SGH[:, c:c + 1]), mg, after_h, n=w)
                    t1 = ve.do(lambda e, r=r, bg=bg, w=w: e.scalar_tensor_tensor(
                        TH[:, r, 0:w], TH[:, r, 0:w], 1.0, bg[:, 0:w], ALU.add, ALU.mult), th, mg, after_h, n=w)
                    h = ve.do(lambda e, c=c, r=r, bu=bu, w=w: e.scalar_tensor_tensor(
                        TH[:, r, 0:w], bu[:, 0:w], SUH[:, c:c + 1], TH[:, r, 0:w], ALU.mult, ALU.mult), mu, t1, n=w)
                    DENSE.free(ig, th, t1)
                else:
                    th = ac.do(lambda e, r=r, bg=bg, w=w: e.activation(TH[:, r, 0:w], bg[:, 0:w], ACT.Tanh,
                                                                       scale=0.5 / XS), mg, after_h, n=w)
                    h = ve.do(lambda e, r=r, bu=bu, w=w: e.scalar_tensor_tensor(
                        TH[:, r, 0:w], TH[:, r, 0:w], 1.0, bu[:, 0:w], ALU.add, ALU.mult), th, mu, after_h, n=w)
                    DENSE.free(ig, th)
                DENSE.free(iu, h)
                if late:
                    split(*late.pop())
                late.append((c, r, w, h))
                yield 1740 / (2 if half else 1), [], DENSE
            XTR.free(n, mu)
            yield 0, [h], None
            split(*late.pop())
            ready_all = list(ready.values())
            yield 0, [ready_all], DENSE
            new = []
            for pair in range(2):
                i, bank, after = DENSE.take()
                pe.expect(ready_all)
                for q in range(2):
                    t = 2 * pair + q
                    z = t // 2
                    steps = [(c, j) for c in range(FC - 1) for j in range(2)] + [(FC - 1, 0)]
                    for s, (c, j) in enumerate(steps):
                        if c < FC - 1:
                            lhs, rhs = HH[j][:, c * T + t * P:c * T + (t + 1) * P], WD[l][:, c, :]
                        else:
                            lhs, rhs = HX[:, z, (t % 2) * P:(t % 2 + 1) * P], WD[l][:, c, :]
                        m = pe.do(lambda e, lhs=lhs, rhs=rhs, bank=bank, q=q, s=s:
                                  e.matmul(bank[:, q * D:(q + 1) * D], lhs, rhs, start=s == 0, stop=s == 10),
                                  ready[c], w_ffn[l], after, inc=s == 10, n=256)
                xv = X[:, NT * b + 2 * pair:NT * b + 2 * pair + 2, :].rearrange("p t n -> p (t n)")
                if l == 0:
                    r, _, after_d = H2.take()
                    sdb = SD[:, :].unsqueeze(1).to_broadcast([P, 2, D])
                    d = ve.do(lambda e, r=r, bank=bank, sdb=sdb: e.scalar_tensor_tensor(
                        TH[:, r, :].rearrange("p (t n) -> p t n", t=2), bank[:, :].rearrange("p (t n) -> p t n", t=2),
                        0.5 / HS, sdb, ALU.mult, ALU.mult), m, after_d)
                    DENSE.free(i, d)
                    y = po.do(lambda e, r=r, xv=xv: e.tensor_tensor(xv, xv, TH[:, r, :], ALU.add), d, x_read)
                    H2.free(r, y)
                else:
                    y = ve.do(lambda e, xv=xv, bank=bank: e.scalar_tensor_tensor(
                        xv, bank[:, :], 0.25 / XS, xv, ALU.mult, ALU.add), m, x_read)
                    DENSE.free(i, y)
                new.append(y)
                yield 2600, [ready_all], DENSE
            ffn_free["HH"] = [m]
            x_ready[b] = new

        Q2 = Ring([0, 1])
        QPR = Ring([0, 1])
        PR = Ring(PB)
        TERMS = [(0, 0), (0, 1), (1, 0)]
        inv = 1.0 / (XS * WS)
        ATT = [(b, l) for l in range(2) for b in range(NB)]
        fronts, valued, cores, tails, quads_done = set(), set(), set(), set(), set()
        att = [{} for _ in ATT]
        free = {"SQ": [[] for _ in range(4)], "SK": [[] for _ in range(4)], "V": [], "MX": [[]] * 4, "NM": [[]] * 4,
                "OT": [[]] * 4, "DC": [[], []], "RB": [[], []], "OC": [[], []], "CH": [],
                "SCR": [[[], []], [[], []]]}

        def khead(n, h):
            return h if n < NB else 4 * (n - NB) + h % 4

        def front(n):
            b, l = ATT[n]
            slot, xt, x_parts, x_read = yield from turn((yield from normalise(b)))
            stacked = att[n]["stacked"] = {}
            att[n].update(slot=slot, xt=xt, x_read=x_read, x_parts=x_parts)
            order = (0, 2, 1, 3) if l == 0 else (2, 0, 1)
            for c in order:
                width = 64 if (l == 1 and c == 2) else P
                i, bank, after = DENSE.take()
                pe.expect(x_parts)
                for s, (jw, jx) in enumerate(TERMS):
                    for k in range(2):
                        m = pe.do(lambda e, c=c, jw=jw, jx=jx, k=k, s=s, width=width, bank=bank: e.matmul(
                            bank[0:width, :], WA[l][:, jw, k, c * P:c * P + width], xt[jx][:, k, :],
                            start=s == 0 and k == 0, stop=s == 2 and k == 1),
                            x_parts[2 * jx + k], w_att[l], after, inc=s == 2 and k == 1)
                rq, _, after_p = QPR.take()
                QP = [QPB[:, rq, j, :] for j in range(2)]
                if l == 0:
                    r, _, after_q = Q2.take()
                    qf = ac.do(lambda e, r=r, bank=bank: e.activation(QF[:, r, :], bank[:, :], ACT.Copy, scale=inv),
                               m, after_q)
                    DENSE.free(i, qf)
                    yield 0, [qf], None
                    sh = ve.do(lambda e, r=r: e.stream_shuffle(QS[:, r, :], QF[:, r, :], [v ^ 8 for v in range(32)]),
                               qf, after_q)
                    s2 = po.do(lambda e, r=r: e.tensor_tensor(QS[:, r, :], QS[:, r, :], ROPE[:, 1, :], ALU.mult),
                               sh, g_c2.done)
                    c2 = ve.do(lambda e, r=r: e.tensor_tensor(QF[:, r, :], QF[:, r, :], ROPE[:, 0, :], ALU.mult),
                               sh, g_c2.done)
                    yield 1300, [s2, c2], None
                    ad = ve.do(lambda e, r=r: e.tensor_tensor(QF[:, r, :], QF[:, r, :], QS[:, r, :], ALU.add), s2, c2)
                    yield 0, [ad], None
                    hi = ac.do(lambda e, r=r, QP=QP: e.activation(QP[0], QF[:, r, :], ACT.Copy), ad, after_p)
                    lo = po.do(lambda e, r=r, QP=QP: e.tensor_tensor(QP[1], QF[:, r, :], QP[0], ALU.subtract),
                               hi, after_p)
                    Q2.free(r, hi, lo)
                else:
                    hi = ac.do(lambda e, width=width, bank=bank, QP=QP: e.activation(
                        QP[0][0:width], bank[0:width, :], ACT.Copy, scale=inv), m, after_p)
                    lo = ve.do(lambda e, width=width, bank=bank, QP=QP: e.scalar_tensor_tensor(
                        QP[1][0:width], bank[0:width, :], inv, QP[0][0:width], ALU.mult, ALU.subtract),
                        hi, after_p)
                    DENSE.free(i, hi, lo)
                is_q = c < 2
                h0 = 8 * (c % 2) if (is_q or l == 0) else 4 * (n - NB)
                nh = 4 if width == 64 else 8
                need = (n - 1 if width == P else NB - 1, (h0 + nh) // 4 - 1)
                while n and need not in quads_done:
                    yield None
                g = group(f"g_st{n}{c}")
                was = free["SQ" if is_q else "SK"]
                before = [was[h0 // 4], was[(h0 + nh - 1) // 4]]
                for blk, j in (((0, 0), (1, 1), (2, 0)) if is_q else ((0, 0), (1, 0), (2, 1))):
                    dst = (SQ if is_q else SK)[16 * blk:16 * blk + 16, h0:h0 + nh, :]
                    sp.dma(dst, QP[j][0:width], g, (hi, lo)[j], before, z_sq, z_k1)
                QPR.free(rq, g.done)
                stacked[c] = g.done
                fronts.add((n, c))
                yield 0 if l == 0 else 1300, [x_parts], DENSE
            fronts.add((n, "all"))

        def values(n):
            b, l = ATT[n]
            xt = att[n]["xt"]
            KH = NH if l == 0 else 4
            v0 = 2 * D if l == 0 else 320
            vw = 16 * KH
            per = min(T // vw, NT)
            got = []
            for t0 in range(0, NT, per):
                i, bank, after = DENSE.take()
                for t in range(t0, t0 + per):
                    for s, (jw, jx) in enumerate(TERMS):
                        for k in range(2):
                            m = pe.do(lambda e, jw=jw, jx=jx, k=k, s=s, t=t, t0=t0, bank=bank: e.matmul(
                                bank[:, (t - t0) * vw:(t - t0 + 1) * vw], xt[jx][:, k, t * P:(t + 1) * P],
                                WA[l][:, jw, k, v0:v0 + vw],
                                start=s == 0 and k == 0, stop=s == 2 and k == 1),
                                att[n]["x_parts"], w_att[l], after, inc=s == 2 and k == 1, n=vw)
                vv = ac.do(lambda e, t0=t0, bank=bank: e.activation(
                    V[:, t0:t0 + per, 0:KH, 0:16],
                    bank[:, 0:per * vw].rearrange("p (t h d) -> p t h d", t=per, h=KH), ACT.Copy, scale=inv),
                    m, free["V"], z_v)
                DENSE.free(i, vv)
                got.append(vv)
                yield 1300, [], DENSE
            XTR.free(att[n]["slot"], m)
            att[n]["v"] = got
            valued.add(n)

        def max_pass(n, g):
            b, l = ATT[n]
            got = []
            stacked = [att[n]["stacked"][c] for c in (g // 2, 2 + g // 2 if l == 0 else 2)]
            for t in range(NT):
                per = [4, 2, 1, 1][t]
                kw = (t + 1) * P
                for h0 in range(0, 4, per):
                    i, bank, after = MAXB.take()
                    for a in range(per):
                        h = 4 * g + h0 + a
                        pe.do(lambda e, a=a, h=h, t=t, kw=kw, bank=bank: e.matmul(
                            bank[:, a * kw:(a + 1) * kw], SQ[0:96, h, t * P:(t + 1) * P],
                            SK[0:96, khead(n, h), 0:kw], start=a == 0, stop=False, skip_group_check=True),
                            stacked, [alibi[g], alibi[n - NB]] if l else None, z_k1, after, inc=False, n=kw)
                    for a in range(per):
                        m = pe.do(lambda e, a=a, t=t, kw=kw, bank=bank: e.matmul(
                            bank[:, a * kw + t * P:(a + 1) * kw], IDH[:, :], MASK[:, 0, :],
                            start=False, stop=True, skip_group_check=True), g_c2.done, inc=a == per - 1, n=P)
                    r = ve.do(lambda e, h0=h0, t=t, per=per, kw=kw, bank=bank: e.tensor_reduce(
                        MX[:, g, h0:h0 + per, t], bank[:, 0:per * kw].rearrange("p (a k) -> p a k", a=per),
                        AX.X, ALU.max, negate=True), m, free["MX"][g], n=per * kw)
                    MAXB.free(i, r)
                    got.append(r)
                    yield 330, [stacked], MAXB
            yield 0, [got], MAXB
            i, bank, after = MAXB.take()
            tr = pe.do(lambda e, bank=bank: e.transpose(bank[0:16, 0:P], MX[:, g, :, :].rearrange("p h t -> p (h t)"),
                                             ID[:, :]), got, after, n=256)
            nm = ac.do(lambda e, bank=bank: e.activation(NM[:, g, :], bank[0:16, 0:P], ACT.Copy), tr, free["NM"][g], n=P)
            MAXB.free(i, nm)
            gr = group(f"g_nm{n}{g}")
            ac.dma(SQ[96:97, 4 * g:4 * g + 4, :].rearrange("o h (t q) -> o (h t) q", t=NT), NM[:, g, :], gr,
                   nm, free["SQ"][g], z_sq)
            free["MX"][g] = [tr]
            free["NM"][g] = [gr.done]
            att[n]["max", g] = gr.done

        PLACE = {(0, 0): 0, (0, 1): T, (0, 3): T + 384, (0, 2): 2 * T, (1, 2): 2 * T + 256,
                 (1, 0): 3 * T, (1, 1): 4 * T, (1, 3): 4 * T + 384}

        def st_pass(n, g):
            b, l = ATT[n]
            slot, pbuf, after_p = PR.take()
            got = []
            wants = att[n]["max", g]
            yield 0, [wants, after_p], STB
            for pr in range(2):
                h = 4 * g + 2 * pr
                todo = [[(0, 0)], [(0, 1), (0, 3)], [(0, 2), (1, 2)], [(1, 0)], [(1, 1), (1, 3)]]
                for s, items in enumerate(todo):
                    i, bank, after = STB.take()
                    for a, kb in items:
                        w = T - kb * P
                        at = PLACE[a, kb] - s * T
                        pe.do(lambda e, a=a, kb=kb, w=w, at=at, bank=bank, h=h: e.matmul(
                            bank[:, at:at + w], SK[0:QROWS, khead(n, h + a), kb * P:(kb + 1) * P],
                            SQ[0:QROWS, h + a, kb * P:T], start=at == 0, stop=False, skip_group_check=True),
                            wants, after, inc=False, n=w)
                    for a, kb in items:
                        at = PLACE[a, kb] - s * T
                        m = pe.do(lambda e, at=at, bank=bank: e.matmul(
                            bank[:, at:at + P], IDH[:, :], MASK[:, 1, :], start=False, stop=True,
                            skip_group_check=True), inc=(a, kb) == items[-1], n=P)
                    ex = ac.do(lambda e, pr=pr, s=s, bank=bank, pbuf=pbuf: e.activation(
                        pbuf[:, pr, s * T:(s + 1) * T], bank[:, :], ACT.Exp, scale=0.25), m, after_p)
                    STB.free(i, ex)
                    got.append(ex)
                    yield 330, [], STB
            free["SQ"][g] = [m]
            free["SK"][g] = [m]
            if n == NB - 1:
                ga = group(f"g_ali{g}")
                sp.dma(SQ[48:54, 4 * g:4 * g + 4, :], alibi_q[:, 4 * g:4 * g + 4, :], ga, m)
                sp.dma(SK[48:54, 4 * g:4 * g + 4, :], alibi_k, ga, m)
                alibi.append(ga.done)
            quads_done.add((n, g))
            att[n]["exp", g] = (slot, pbuf, got)

        def pv_pass(n, g):
            b, l = ATT[n]
            slot, pbuf, got = att[n]["exp", g]
            yield 0, [got, att[n]["v"]], PVB
            i, bank, after = PVB.take()
            pe.expect(got, att[n]["v"])
            for kb in range(NT):
                for a in range(4):
                    at = PLACE[a % 2, kb]
                    w = T - kb * P
                    m = pe.do(lambda e, a=a, kb=kb, at=at, w=w: e.matmul(
                        bank[32 * a:32 * a + 32, kb * P:T], V[:, kb, 4 * g + a if l == 0 else a, :],
                        pbuf[:, a // 2, at:at + w], start=kb == 0, stop=kb == NT - 1),
                        got[5 * (a // 2) + at // T], att[n]["v"], z_v, after, inc=kb == NT - 1 and a == 3, n=w)
                yield 900 - 200 * kb, [], None
            PR.free(slot, m)
            o = ac.do(lambda e: e.activation(OT[:, g, :], bank[:, :], ACT.Copy), m, free["OT"][g])
            PVB.free(i, o)
            att[n]["o", g] = o
            if g == 3:
                free["V"] = [m]

        def max_stream():
            for n in range(len(ATT)):
                l = ATT[n][1]
                for g in range(4):
                    while any((n, c) not in fronts for c in (g // 2, 2 + g // 2 if l == 0 else 2)):
                        yield None
                    while n and (n - 1, g) not in quads_done:
                        yield None
                    yield from max_pass(n, g)

        def st_stream():
            for n in range(len(ATT)):
                for g in range(4):
                    while not prepared or ("max", g) not in att[n] or not PR.idle:
                        yield None
                    yield from st_pass(n, g)

        def pv_stream():
            for n in range(len(ATT)):
                while (n, "all") not in fronts:
                    yield None
                yield from values(n)
                for g in range(4):
                    while (n, g) not in quads_done or (n and n - 1 not in tails):
                        yield None
                    yield from pv_pass(n, g)
                cores.add(n)

        def tail(n):
            b, l = ATT[n]
            c_ready, inverse = {}, []
            if l == 1:
                xb = X[:, NT * b:NT * b + NT, :]
                att[n]["x_read"] = [po.do(lambda e: e.tensor_tensor(
                    xb, xb, BO[:, :].unsqueeze(1).to_broadcast([P, NT, D]), ALU.add), att[n]["x_read"], g_a0.done, n=1024)]
            for u in range(2):
                while ("o", 2 * u + 1) not in att[n]:
                    yield None
                outs = [att[n]["o", g] for g in (2 * u, 2 * u + 1)]
                yield 0, [outs], None
                g_dc = group(f"g_dc{u}")
                dc = DC[64 * u:64 * u + 64, :]
                sp.dma(dc, OT[16:P:32, 2 * u:2 * u + 2, :].rearrange("a g (s t) -> a (g s) t", t=64), g_dc,
                       outs, free["DC"][u])
                g_oc = group(f"g_oc{u}")
                for a in range(4):
                    sp.dma(OC[32 * a:32 * a + 32, u, :], OT[32 * a:32 * a + 16, 2 * u:2 * u + 2, :], g_oc,
                           outs, free["OC"][u])
                free["OT"][2 * u] = free["OT"][2 * u + 1] = [g_dc.done, g_oc.done]
                yield 0, [g_dc.done], None
                rc = ve.do(lambda e, dc=dc: e.reciprocal(dc, dc), g_dc.done, n=390)
                g_so = group(f"g_so{u}")
                sp.dma(scratch[n % 2, u], dc, g_so, rc, free["SCR"][n % 2][u])
                if g_so not in stores:
                    stores.append(g_so)
                g_si = group(f"g_si{u}")
                for a in range(4):
                    src = scratch[n % 2, u, 16 * a:16 * a + 16, :].rearrange("(o s) t -> o (s t)", o=1)
                    sp.dma(RB[32 * a:32 * a + 32, u, :], src.to_broadcast([16, 2 * T]), g_si, g_so.done, free["RB"][u])
                free["DC"][u] = [g_so.done]
                free["SCR"][n % 2][u] = [g_si.done]
                inverse.append([g_si.done, g_oc.done])
            for u, ready in enumerate(inverse):
                yield 0, [ready], None
                cc = po.do(lambda e, u=u: e.tensor_tensor(OC[:, u, :], OC[:, u, :], RB[:, u, :], ALU.mult), ready)
                free["RB"][u] = [cc]
                yield 0, [cc], None
                hi = ac.do(lambda e, u=u: e.activation(CH[0][:, u, :], OC[:, u, :], ACT.Copy, scale=CS), cc, free["CH"])
                lo = ve.do(lambda e, u=u: e.scalar_tensor_tensor(
                    CH[1][:, u, :], OC[:, u, :], CS, CH[0][:, u, :], ALU.mult, ALU.subtract), hi, cc, free["CH"])
                c_ready[0, u], c_ready[1, u] = hi, lo
                free["OC"][u] = [hi, lo]
            c_all = list(c_ready.values())
            yield 0, [c_all], DENSE
            tails.add(n)
            new = []
            for pair in range(2):
                i, bank, after = DENSE.take()
                pe.expect(c_all)
                for q in range(2):
                    t = 2 * pair + q
                    steps = [(g, jc, jw) for jc, jw in TERMS for g in range(2)]
                    for s, (g, jc, jw) in enumerate(steps):
                        m = pe.do(lambda e, g=g, jc=jc, jw=jw, t=t, q=q, s=s, bank=bank: e.matmul(
                            bank[:, q * D:(q + 1) * D], CH[jc][:, g, t * P:(t + 1) * P], WO[l][:, jw, g, :],
                            start=s == 0, stop=s == 5), c_ready[jc, g], w_att[l], after, inc=s == 5, n=256)
                xv = X[:, NT * b + 2 * pair:NT * b + 2 * pair + 2, :].rearrange("p t n -> p (t n)")
                y = ve.do(lambda e, xv=xv, bank=bank: e.scalar_tensor_tensor(
                    xv, bank[:, :], 1.0 / (CS * WS), xv, ALU.mult, ALU.add), m, att[n]["x_read"])
                DENSE.free(i, y)
                new.append(y)
                yield 1300, [], DENSE
            free["CH"] = [m]
            x_ready[b] = new
            state[b] = ("A", l)

        alibi, prepared, normals, ffns_done = [], set(), {}, []
        state = {}

        def fronts_stream():
            for n, (b, l) in enumerate(ATT):
                while w_att[l] is None or state.get(b) != ("F", l) or (n and n - 1 not in valued):
                    yield None
                yield from front(n)

        first = [(b, 0, None, ("F", 0)) for b in range(NB)]
        mid0 = [(b, 0, ("A", 0), ("M", 0)) for b in range(NB)]
        mid1 = [(b, 1, ("M", 0), ("F", 1)) for b in range(NB)]
        final = [(b, 1, ("A", 1), ("E", 1)) for b in range(NB)]
        FFNS = first + mid0[:1] + [f for pair in zip(mid1, mid0[1:]) for f in pair] + mid1[3:] + final
        GATES = [0, 0, 2, 2, 7, 5, 12, 13, 15, 17, 19, 22, 23, 24, 32, 29]

        def norms_stream():
            for (b, l, before, _), gate in zip(FFNS, GATES):
                while len(quads_done) < gate or state.get(b) != before or any(normals.values()):
                    yield None
                normals[b, l] = [(yield from normalise(b, l == 0))]

        def ffn_stream(first, end):
            while len(ffns_done) < first:
                yield None
            for b, l, before, says in FFNS[first:end]:
                yield from ffn(b, l)
                state[b] = says
                ffns_done.append((b, l))
                if says == ("E", 1):
                    g = group(f"g_out{b}")
                    sp.dma(out[:, NT * b:NT * b + NT, :], X[:, NT * b:NT * b + NT, :], g, x_ready[b])
                    stores.append(g)

        def tails_stream():
            for n in range(len(ATT)):
                yield from tail(n)

        def prepare():
            yield 100, [g_s0.done], None
            w_sg = ve.do(lambda e: e.tensor_scalar(SGH[:, :], SGU[:, 0, :], 0.5 / XS, None, ALU.mult), g_s0.done, n=6)
            w_su = ve.do(lambda e: e.scalar_tensor_tensor(SUH[:, :], SGU[:, 0, :], 0.5 * HS / (XS * XS),
                                                          SGU[:, 1, :], ALU.mult, ALU.mult), n=6)
            w_ffn[0] += [w_sg, w_su]
            yield 100, [g_a0.done], None
            w_att[0] = attention_weights(0, g_a0.done)
            yield 100, [], None
            yield from ternary_weights()
            g = group("g_a1")
            sp.dma(ra[1], wqkv1, g)
            sp.dma(ro[1], wo1, g)
            yield 100, [g.done], None
            w_att[1] = attention_weights(1, g.done)
            read = [w_ffn[1], w_att[0], w_att[1]]
            PR.idle = [(i, read) for i in range(2)]
            free["OT"] = [read] * 4
            free["RB"] = [read, read]
            prepared.add(0)

        shares = {"st": [1.663, 1.315, 0.405],
                  "max": [0.117, 0.117, 0.117],
                  "pv": [0.046, 0.048, 0.048],
                  "front": [0.147, 0.147, 0.147],
                  "tail": [1.078, 1.078, 1.078],
                  "norm": [0.266, 0.266, 0.266],
                  "ffn": [0.297, 0.297, 0.297],
                  "last": [0.004, 0.003, 0.004],
                  "prepare": [0.515, 0.515, 0.515]}

        def phase():
            return 0 if len(quads_done) < 2 else 1 if len(quads_done) < 26 else 2

        streams = {"st": st_stream(), "max": max_stream(), "pv": pv_stream(), "front": fronts_stream(), "tail": tails_stream(),
                   "norm": norms_stream(), "ffn": ffn_stream(0, 12), "last": ffn_stream(12, 16), "prepare": prepare()}
        interleave(pe, phase, {n: (shares[n], g) for n, g in streams.items()})

        sp.wait([g.done for g in stores])

        block = ctx.enter_context(nc.Block())

        @block.sync
        def _(e):
            sp.replay(e)

        @block.tensor
        def _(e):
            pe.replay(e)

        @block.vector
        def _(e):
            ve.replay(e)

        @block.scalar
        def _(e):
            ac.replay(e)

        @block.gpsimd
        def _(e):
            po.replay(e)


def kernel(**inputs):
    import numpy as np
    import concourse.bacc as bacc
    from concourse.bass_utils import run_bass_kernel_spmd

    a = {k: np.asarray(v) for k, v in inputs.items()}

    def rows(w):
        return np.ascontiguousarray(w.reshape(2, P, -1).transpose(1, 0, 2))

    def hidden(w):
        full = w[:640].reshape(5, P, -1)
        last = np.concatenate([w[640:], w[640:]], 0)[None]
        return np.ascontiguousarray(np.concatenate([full, last], 0).transpose(1, 0, 2))

    p = np.arange(P)
    perm8 = (p & 7) * 16 + ((p >> 3) & 1) * 8 + (p >> 4)
    q4 = np.arange(64)
    perm4 = (q4 & 3) * 16 + (q4 >> 2)
    perm8b = (p & 7) * 16 + (p >> 3)

    def heads(w):
        o = w.reshape(2, 2, 4, 16, D).transpose(2, 3, 1, 0, 4)
        return np.ascontiguousarray(o.reshape(P, 2, D))

    wq, wk = a["L0_attn_Wq"].T, a["L0_attn_Wk"].T
    qkv0 = np.concatenate([wq[:, perm8], wq[:, P + perm8], wk[:, perm8], wk[:, P + perm8], a["L0_attn_Wv"].T], 1)
    wq, wkv = a["L1_attn_Wq"], a["L1_attn_Wkv"]
    qkv1 = np.concatenate([wq[:, perm8b], wq[:, P + perm8b], wkv[:, perm4], wkv[:, 64:]], 1)

    t = np.arange(T, dtype=np.float32)
    inv_freq = (1.0 / np.float32(10000.0) ** (np.arange(0, 16, 2, dtype=np.float32) / np.float32(16))).astype(np.float32)
    ang = (t[None, :] * inv_freq[p >> 4][:, None]).astype(np.float32)
    sign = np.where((p >> 3) & 1, 1.0, -1.0)[:, None]
    rope = np.stack([np.cos(ang.astype(np.float64)), sign * np.sin(ang.astype(np.float64))], 1).astype(np.float32)

    import ml_dtypes
    qk = np.arange(P)
    m0 = np.where(qk[None, :] > qk[:, None], -1e30, 0.0)
    mask = np.stack([m0, m0.T], 1).astype(ml_dtypes.bfloat16)
    ident = np.eye(P, dtype=np.float32)

    start = 2.0 ** (-2.0 ** (-(np.log2(16) - 3.0)))
    slopes = np.array([start ** (i + 1) for i in range(16)], np.float32).astype(np.float64) * 4.0

    def three(v):
        out = []
        for _ in range(3):
            h = v.astype(np.float16)
            out.append(h)
            v = v - h.astype(np.float64)
        return out

    sl = three(np.broadcast_to(slopes[:, None], (16, T)).astype(np.float64))
    sq = three(-slopes[:, None] * np.arange(T)[None, :])
    alibi_q = np.ascontiguousarray(np.stack(sl + sq, 0))
    kk = np.broadcast_to(np.arange(T).astype(np.float16), (4, T))
    alibi_k = np.ascontiguousarray(np.stack([kk] * 3 + [np.ones((4, T), np.float16)] * 3, 0))

    x = a["L0_attn_hidden_states"].reshape(NB * NT, P, D).transpose(1, 0, 2)
    sgu = np.stack([hidden(a["L0_ffn_s_gate"][:, None])[:, :, 0], hidden(a["L0_ffn_s_up"][:, None])[:, :, 0]], 1)
    arrays = {
        "x_in": x,
        "wqkv0": rows(qkv0),
        "wo0": heads(a["L0_attn_Wo"].T),
        "gu0": rows(np.concatenate([a["L0_ffn_wq_gate"].T, a["L0_ffn_wq_up"].T], 1)),
        "sgu0": sgu,
        "wd0": hidden(a["L0_ffn_wq_down"].T),
        "sd0": np.broadcast_to(a["L0_ffn_s_down"][None], (P, D)),
        "wqkv1": rows(qkv1),
        "wo1": heads(a["L1_attn_Wo"]),
        "gu1": rows(np.concatenate([a["L1_ffn_w1"].T, a["L1_ffn_w2"].T], 1)),
        "wd1": hidden(a["L1_ffn_w3"].T),
        "rope": rope,
        "mask": mask,
        "ident": ident,
        "identh": ident.astype(ml_dtypes.bfloat16),
        "alibi_q": alibi_q,
        "alibi_k": alibi_k,
        "bo1": np.broadcast_to(a["L1_attn_bo"][None], (P, D)),
    }
    arrays = {k: np.ascontiguousarray(v) for k, v in arrays.items()}
    nc = bacc.Bacc("TRN2", target_bir_lowering=False, num_devices=1)
    args = [nc.dram_tensor(k, v.shape, mybir.dt.from_np(v.dtype), kind="ExternalInput").ap() for k, v in arrays.items()]
    scratch = nc.dram_tensor("scratch", (2, 2, 64, 64), F32, kind="Internal").ap()
    out = nc.dram_tensor("out", (P, NB * NT, D), F32, kind="ExternalOutput").ap()
    macaron_kernel(nc, *args, scratch, out)
    r = run_bass_kernel_spmd(nc, [arrays], core_ids=[0])
    y = np.asarray(r.results[0]["out"])
    return np.ascontiguousarray(y.transpose(1, 0, 2)).reshape(NB, T, D)
```
